# Optimizing a Trainium2 kernel written in Bass

```python
import numpy as np
import jax
import jax.numpy as jnp

def _softmax(x, axis=-1):
    return jax.nn.softmax(x, axis=axis)

def _gelu(x):
    return jax.nn.gelu(x, approximate=True)

def _silu(x):
    return jax.nn.silu(x)

def _sigmoid(x):
    return jax.nn.sigmoid(x)

def _layernorm(x, axis=-1, eps=1e-05):
    m = jnp.mean(x, axis=axis, keepdims=True)
    v = jnp.var(x, axis=axis, keepdims=True)
    return (x - m) / jnp.sqrt(v + eps)

def _scatter_add(tgt, idx, src, axis=0):
    return tgt.at[idx].add(src)

def _segment_sum(src, seg, n):
    return jax.ops.segment_sum(src, seg, n)
kernel_name = 'mk_hybrid_d1_jaxref_r8_364c13'

def setup_inputs(seed: int=0):
    np.random.seed(seed)
    _w = jnp.asarray

    def _L0_attn_a_setup():
        import math
        import jax, jax.numpy as jnp
        import numpy as np
        IN_F, OUT_F, HID = (512, 512, 512)
        WINDOW, STRIPES = (6, 3)

        def make_sparse_mask(n_in=IN_F, n_out=OUT_F, window=WINDOW, stripes=STRIPES):
            m = np.zeros((n_in, n_out), dtype=np.float32)
            stride = int(math.sqrt(n_in))
            for k in range(stripes):
                ps = stride * k
                for i in range(0, n_in, window):
                    m[ps + i:ps + i + window, i:i + window] = 1.0
            mb = m.astype(bool)
            return jnp.asarray((mb | mb.T).astype(np.float32))
        key = jax.random.key(seed)
        k1, k2, k3, k4 = jax.random.split(key, 4)
        scale = 1.0 / math.sqrt(IN_F)
        x = jax.random.normal(k1, (8, 96, IN_F), dtype=jnp.float32)
        w1 = jax.random.normal(k2, (HID, IN_F), dtype=jnp.float32) * scale
        w2 = jax.random.normal(k3, (OUT_F, HID), dtype=jnp.float32) * scale
        b2 = jax.random.normal(k4, (OUT_F,), dtype=jnp.float32) * scale
        return {'x': x, 'w1': w1, 'w2': w2, 'b2': b2, 'sparse_mask': make_sparse_mask()}
    _L0_attn_a_in = _L0_attn_a_setup()

    def _L0_attn_b_setup():
        import jax, jax.numpy as jnp
        import numpy as np
        H = 512
        D = H // 4
        key = jax.random.key(seed)
        k1, k2, k3, k4, k5 = jax.random.split(key, 5)
        x = jax.random.normal(k1, (4, 512, H), dtype=jnp.float32)
        s_in = 1.0 / np.sqrt(H)
        Wqkv = jax.random.normal(k2, (H, 3 * D), dtype=jnp.float32) * s_in
        bqkv = jax.random.normal(k3, (3 * D,), dtype=jnp.float32) * 0.01
        Wo = jax.random.normal(k4, (D, H), dtype=jnp.float32) * (1.0 / np.sqrt(D))
        bo = jax.random.normal(k5, (H,), dtype=jnp.float32) * 0.01
        return {'x': x, 'Wqkv': Wqkv, 'bqkv': bqkv, 'Wo': Wo, 'bo': bo}
    _L0_attn_b_in = _L0_attn_b_setup()

    def _L0_ffn_setup():
        import jax, jax.numpy as jnp
        import numpy as np
        IN_F = 512
        OUT_F = 512
        N_CLUSTERS = 64
        THRESHOLD = 0.01
        TEMPERATURE = 0.1
        BATCH, SEQ = (4, 256)
        key = jax.random.key(seed)
        k1, k2, k3, k4, k5 = jax.random.split(key, 5)
        s = 1.0 / np.sqrt(IN_F)
        return {'input': jax.random.normal(k1, (BATCH, SEQ, IN_F), dtype=jnp.float32), 'weight': jax.random.normal(k2, (OUT_F, IN_F), dtype=jnp.float32) * s, 'bias': jax.random.uniform(k3, (OUT_F,), dtype=jnp.float32, minval=-s, maxval=s), 'centroids': jax.random.normal(k4, (N_CLUSTERS, IN_F), dtype=jnp.float32) * s, 'assignments': jax.random.randint(k5, (OUT_F,), 0, N_CLUSTERS, dtype=jnp.int32)}
    _L0_ffn_in = _L0_ffn_setup()
    _d = {'L0_attn_a_x': _L0_attn_a_in['x'], 'L0_attn_a_w1': _L0_attn_a_in['w1'], 'L0_attn_a_w2': _L0_attn_a_in['w2'], 'L0_attn_a_b2': _L0_attn_a_in['b2'], 'L0_attn_a_sparse_mask': _L0_attn_a_in['sparse_mask'], 'L0_attn_b_Wqkv': _L0_attn_b_in['Wqkv'], 'L0_attn_b_bqkv': _L0_attn_b_in['bqkv'], 'L0_attn_b_Wo': _L0_attn_b_in['Wo'], 'L0_attn_b_bo': _L0_attn_b_in['bo'], 'L0_ffn_weight': _L0_ffn_in['weight'], 'L0_ffn_bias': _L0_ffn_in['bias'], 'L0_ffn_centroids': _L0_ffn_in['centroids'], 'L0_ffn_assignments': _L0_ffn_in['assignments']}
    _x0 = _d['L0_attn_a_x']
    _d['L0_attn_a_x'] = jax.random.normal(jax.random.fold_in(jax.random.key(seed), 1), (4, 512, 512), dtype=_x0.dtype)
    del _x0
    return _d

def reference(L0_attn_a_x, L0_attn_a_w1, L0_attn_a_w2, L0_attn_a_b2, L0_attn_a_sparse_mask, L0_attn_b_Wqkv, L0_attn_b_bqkv, L0_attn_b_Wo, L0_attn_b_bo, L0_ffn_weight, L0_ffn_bias, L0_ffn_centroids, L0_ffn_assignments):

    def _L0_attn_a_ref(x, w1, w2, b2, sparse_mask):
        import math
        import jax, jax.numpy as jnp
        import numpy as np
        IN_F, OUT_F, HID = (512, 512, 512)
        WINDOW, STRIPES = (6, 3)

        def make_sparse_mask(n_in=IN_F, n_out=OUT_F, window=WINDOW, stripes=STRIPES):
            m = np.zeros((n_in, n_out), dtype=np.float32)
            stride = int(math.sqrt(n_in))
            for k in range(stripes):
                ps = stride * k
                for i in range(0, n_in, window):
                    m[ps + i:ps + i + window, i:i + window] = 1.0
            mb = m.astype(bool)
            return jnp.asarray((mb | mb.T).astype(np.float32))
        attn = jnp.einsum('ds,td->st', w1, w2) * sparse_mask
        y = jnp.einsum('bds,st->bdt', x, attn) + b2
        return jax.nn.gelu(y, approximate=False)

    def _L0_attn_b_ref(x, Wqkv, bqkv, Wo, bo):
        import jax, jax.numpy as jnp
        import numpy as np
        H = 512
        D = H // 4
        B, S, C = x.shape
        d = C // 4
        qkv = jnp.einsum('bsc,cf->bsf', x, Wqkv) + bqkv
        qkv = qkv.reshape(B, S, 3, d)
        q, k, v = (qkv[:, :, 0], qkv[:, :, 1], qkv[:, :, 2])
        scale = 1.0 / jnp.sqrt(jnp.float32(d)).astype(x.dtype)
        attn = jnp.einsum('bqd,bkd->bqk', q, k) * scale
        attn = jax.nn.softmax(attn, axis=-1)
        out = jnp.einsum('bqk,bkd->bqd', attn, v)
        return jnp.einsum('bqd,dc->bqc', out, Wo) + bo

    def _L0_ffn_ref(input, weight, bias, centroids, assignments):
        import jax, jax.numpy as jnp
        import numpy as np
        IN_F = 512
        OUT_F = 512
        N_CLUSTERS = 64
        THRESHOLD = 0.01
        TEMPERATURE = 0.1
        BATCH, SEQ = (4, 256)
        shape = input.shape
        x = input.reshape(-1, shape[-1])
        dots = jax.nn.softmax(x @ centroids.T / TEMPERATURE, axis=-1)
        hits = dots > THRESHOLD
        query_sel = jnp.any(hits, axis=1)
        cluster_sel = jnp.any(hits, axis=0)
        row_sel = cluster_sel[assignments]
        dense = x @ weight.T + bias
        out = jnp.where(query_sel[:, None] & row_sel[None, :], dense, jnp.zeros((), dense.dtype))
        return out.reshape(*shape[:-1], -1)
    x = L0_attn_a_x
    x = x + _L0_attn_a_ref(_layernorm(x, axis=-1), L0_attn_a_w1, L0_attn_a_w2, L0_attn_a_b2, L0_attn_a_sparse_mask)
    x = x + _L0_ffn_ref(_layernorm(x, axis=-1), L0_ffn_weight, L0_ffn_bias, L0_ffn_centroids, L0_ffn_assignments)
    x = x + _L0_attn_b_ref(_layernorm(x, axis=-1), L0_attn_b_Wqkv, L0_attn_b_bqkv, L0_attn_b_Wo, L0_attn_b_bo)
    x = x + _L0_ffn_ref(_layernorm(x, axis=-1), L0_ffn_weight, L0_ffn_bias, L0_ffn_centroids, L0_ffn_assignments)
    return x

_drawn_inputs = setup_inputs


def setup_inputs(seed=0):
    import zlib

    import numpy as np

    out = dict(_drawn_inputs(seed))
    spreads = {}
    factors = {'L0_attn_b_bqkv': 8.0, 'L0_attn_b_bo': 8.0}
    for name, (base, spread) in spreads.items():
        noise = np.random.default_rng([zlib.crc32(name.encode()), seed]).standard_normal(out[name].shape)
        drawn = base * np.exp(spread * noise) if base else spread * noise
        out[name] = jnp.asarray(drawn.astype(out[name].dtype))
    for name, factor in factors.items():
        out[name] = (out[name] * factor).astype(out[name].dtype)
    return out
```

```python
from contextlib import ExitStack

import concourse.bass as bass
from concourse import mybir

F32 = mybir.dt.float32
F32R = mybir.dt.float32r
I32 = mybir.dt.int32
ALU = mybir.AluOpType
ACT = mybir.ActivationFunctionType
AX = mybir.AxisListType

P = 128
NB, S, D = 4, 512, 512
TPB = S // P
NT = NB * TPB
KC = D // P
DH = D // 4
NC = 64
EPS = 1e-5
THRESHOLD = 0.01
INV_TEMPERATURE = 10.0
SCALE = float(DH) ** -0.5
T_BANKS = 4
M_BANKS = 4

FREED_BY_VECTOR = ("attn", "q", "k", "pv", "wo")


def schedule():
    o = []

    def step(*s):
        o.append(s)

    def transposed(what, b, t):
        step("T", what, b, t)
        step("lo", what, b, t)

    def residual(what, stage, b, t):
        step(what, "", b, t)
        step("stats", stage, b, t)
        step("norm", stage, b, t)

    for c in range(KC):
        step("T", "w2", 0, c)
        step("w1", "", 0, c)
        step("lo", "w2", 0, c)
    for t in range(TPB):
        step("stats", 1, 0, t)
        step("norm", 1, 0, t)
        step("M", "attn", 0, t)
        if t:
            step("split_attn", "", 0, t - 1)
            transposed("x1", 0, t - 1)
        step("mask_attn", "", 0, t)
    step("biases", "", 0, 0)
    transposed("x1", 0, TPB - 1)
    step("split_attn", "", 0, TPB - 1)
    for t in range(TPB):
        step("stats", 1, 1, t)
        step("norm", 1, 1, t)
        step("T", "ffn", 0, t)
        step("M", "y1", 0, t)
        step("lo", "ffn", 0, t)
        if t:
            transposed("x1", 1, t - 1)
            residual("x1", 2, 0, t - 1)
    transposed("cen", 0, 0)
    transposed("x1", 1, TPB - 1)

    for b in range(1, NB):
        for t in range(TPB):
            ahead = t + (b > 1)
            if ahead < TPB:
                step("T", "x2", b - 1, ahead)
            step("M", "y1", b, t)
            if t:
                residual("x1", 2, b, t - 1)
            elif b == 1:
                residual("x1", 2, 0, TPB - 1)
            if ahead < TPB:
                step("lo", "x2", b - 1, ahead)
            if b + 1 < NB:
                step("stats", 1, b + 1, t)
                step("norm", 1, b + 1, t)
        step("M", "cl2", b - 1, 0)
        residual("x1", 2, b, TPB - 1)
        if b + 1 < NB:
            for t in range(TPB):
                step("T", "x1", b + 1, t)
                if t == TPB - 1:
                    step("T", "x2", b, 0)
                step("M", "dn2", b - 1, t)
                step("lo", "x1", b + 1, t)
                if t == TPB - 1:
                    step("lo", "x2", b, 0)
                if t == 0:
                    step("T", "tc2", b - 1, 0)
                    step("logit2", "", b - 1, 0)
                if t == 2:
                    step("prob2", "", b - 1, 0)
    clustered(step, transposed, 2, "x3")
    for t in range(TPB):
        residual("x2", 3, 0, t)
        transposed("x3", 0, t)

    for b in range(NB):
        step("M", "q", b, 0)
        if b:
            transposed("x4", b - 1, 0)
        step("M", "k", b, 0)
        step("lo_q", "", b, 0)
        if b:
            transposed("x4", b - 1, 1)
        step("M", "v", b, 0)
        step("lo_k", "", b, 0)
        if b:
            transposed("x4", b - 1, 2)
            transposed("x4", b - 1, 3)
        for t in range(TPB):
            step("M", "sc", b, t)
            step("exp", "", b, t)
            if t == 1:
                transposed("v", b, 0)
        if b:
            step("M", "cl4", b - 1, 0)
        for t in range(TPB):
            step("T", "p", b, t)
            if b and (b < NB - 1 or t < 1) and t < TPB - 1:
                step("M", "dn4", b - 1, t)
            step("lo", "p", b, t)
            if b and t == 1:
                step("T", "tc4", b - 1, 0)
                step("logit4", "", b - 1, 0)
            if b and t == 2:
                step("prob4", "", b - 1, 0)
            if b + 1 < NB:
                residual("x2", 3, b + 1, t)
                if t:
                    transposed("x3", b + 1, t - 1)
        step("M", "pv", b, 0)
        if b + 1 < NB:
            step("T", "x3", b + 1, TPB - 1)
            if b:
                step("M", "dn4", b - 1, TPB - 1)
            step("lo", "x3", b + 1, TPB - 1)
        step("lo_o", "", b, 0)
        for t in range(TPB):
            step("M", "wo", b, t)
        for t in range(TPB):
            residual("x3", 4, b, t)
    clustered(step, transposed, 4, None)
    for n in range(NT):
        step("out", "", *divmod(n if n < NT - 2 * TPB else NT - 3 * TPB + n if n < NT - TPB else n - TPB, TPB))
    return o


def clustered(step, transposed, stage, following):
    b, what = NB - 1, f"x{stage}"
    dense, clusters = f"dn{stage}", f"cl{stage}"
    if stage == 4:
        step("M", dense, b - 1, 1)
    for t in range(TPB):
        if stage == 2 and t < 2:
            step("M", dense, b - 1, t)
        transposed(what, b, t)
        if stage == 2 and t == 1:
            step("T", "tc2", b - 1, 0)
            step("logit2", "", b - 1, 0)
            step("prob2", "", b - 1, 0)
    step("M", clusters, b, 0)
    step("M", dense, b, 0)
    step("T", f"tc{stage}", b, 0)
    step(f"logit{stage}", "", b, 0)
    step("M", dense, b, 1)
    step(f"prob{stage}", "", b, 0)
    step("M", dense, b, 2)
    step(f"best{stage}", "", 0, 0)
    step("M", dense, b, 3)
    step(f"mask{stage}", "", 0, 0)
    step("M", dense, b - 1, 2)
    step("M", dense, b - 1, 3)


def masked_by_vector(kind, _, b, t):
    return b * TPB + t < TPB and t % 2 == 0 if kind == "x2" else t % TPB == 2


def program(nc, x_d, w1_d, w2_d, b2_d, sparse_d, wqkv_d, bqkv_d, wo_d, bo_d, ffn_d, fb_d, cen_d,
            assign_d, out_d):
    STEPS = schedule()
    T_AT = {}
    M_AT = {}
    for s in STEPS:
        if s[0] == "T":
            T_AT[s[1:]] = len(T_AT)
        if s[0] in ("best2", "best4"):
            T_AT[s[0], 0, 0] = len(T_AT)
        if s[0] in ("mask2", "mask4"):
            M_AT[s[0], 0, 0] = len(M_AT)
        if s[0] == "M":
            M_AT[s[1:]] = len(M_AT)
    M_JOBS = list(M_AT)
    STAT_AT = {s[1:]: n for n, s in enumerate([s for s in STEPS if s[0] == "stats"])}
    MASK_AT = {s: n for n, s in enumerate([s for s in STEPS if s[0] in ("x2", "out") and not masked_by_vector(*s)])}
    NORM_AT = {s[1:]: n for n, s in enumerate([s for s in STEPS if s[0] == "norm"])}
    HI_JOBS = [j for j in T_AT if j[0] not in ("tc2", "tc4", "best2", "best4")]
    HI_AT = {j: n for n, j in enumerate(HI_JOBS)}
    SOFT = [(s[0][-1], s[2]) for s in STEPS if s[0] in ("logit2", "logit4")]

    assert list(T_AT.values()) == [T_AT[j] for j in [
        (s[1:] if s[0] == "lo" else ("tc" + s[0][-1], s[2], 0) if s[0] in ("logit2", "logit4") else (s[0], 0, 0))
        for s in STEPS if s[0] in ("lo", "logit2", "logit4", "best2", "best4")]]

    ctx = ExitStack()
    with ctx:
        def sb(name, shape, dt=F32):
            return ctx.enter_context(nc.sbuf_tensor(name, shape, dt))

        def sem(name):
            return ctx.enter_context(nc.semaphore(name))

        x_tok = sb("x_tok", [P, NT, D])
        y_tok = sb("y_tok", [P, NT, D])
        odd_hi = sb("odd_hi", [P, KC, S], F32R)
        odd_lo = sb("odd_lo", [P, KC, S], F32R)
        even_hi = sb("even_hi", [P, KC, S], F32R)
        even_lo = sb("even_lo", [P, KC, S], F32R)
        xn_odd = sb("xn_odd", [P, TPB, D])
        xn_even = sb("xn_even", [P, TPB, D])
        w2_raw = sb("w2_raw", [P, KC, D])
        w1_raw = y_tok[:, KC:2 * KC, :]
        ffn_raw = w2_raw
        w1_hi, w1_lo = even_hi, even_lo
        w2t_hi = sb("w2t_hi", [P, KC, D], F32R)
        w2t_lo = sb("w2t_lo", [P, KC, D], F32R)
        pt_hi, pt_lo = w2t_hi, w2t_lo
        sparse = y_tok[:, NT - 2 * KC:NT - KC, :]
        attn_f = y_tok[:, NT - KC:NT, :]
        attn_hi = sb("attn_hi", [P, KC, D], F32R)
        attn_lo = sb("attn_lo", [P, KC, D], F32R)
        ffn_hi = sb("ffn_hi", [P, KC, D], F32R)
        ffn_lo = sb("ffn_lo", [P, KC, D], F32R)
        cen_hl = sb("cen_hl", [P, KC, 2 * NC], F32R)
        wqkv_raw = y_tok[:, 2 * KC:3 * KC, 0:3 * DH]
        wo_raw = y_tok[:, NT - 3, :]
        wqkv_hi = sb("wqkv_hi", [P, KC, 3 * DH], F32R)
        wqkv_lo = sb("wqkv_lo", [P, KC, 3 * DH], F32R)
        wo_hi = sb("wo_hi", [P, D], F32R)
        wo_lo = sb("wo_lo", [P, D], F32R)
        p_tok = w2_raw
        gelu = y_tok[:, NT - 2:NT, :]
        q_hi = attn_hi[:, 0, :]
        q_lo = attn_hi[:, 1, :]
        k_hi = attn_hi[:, 2, :]
        k_lo = attn_hi[:, 3, :]
        v_hi = attn_lo[:, 0, :]
        v_lo = attn_lo[:, 1, :]
        o_hi = attn_lo[:, 2, :]
        o_lo = attn_lo[:, 3, :]
        vt = sb("vt", [P, S])
        lg = sb("lg", [P, S])
        cen_raw = lg[0:NC, :]
        cl = sb("cl", [P, TPB, NC])
        ce = sb("ce", [P, TPB, NC])
        best = sb("best", [P, TPB, NC])
        best1 = sb("best1", [P, NC])
        onehot = sb("onehot", [P, D], F32R)
        assign = y_tok[:, 2, :].bitcast(I32)
        cluster = sb("cluster", [P, 1])
        csel = sb("csel", [P, P], F32R)
        csel1 = sb("csel1", [NC, 1])
        rows = sb("rows", [P, D])
        ident = sb("ident", [P, P])
        ones = sb("ones", [P, P], F32R)
        bias1 = sb("bias1", [P, D], F32R)
        bias2 = sb("bias2", [P, D], F32R)
        bias_raw = y_tok[0:33, 0:2, :]
        bqkv = sb("bqkv", [P, 3])
        bo = sb("bo", [P, D])
        half = sb("half", [P, 1])
        st = sb("st", [P, 2, 6])
        mv = sb("mv", [P, 4 * NT, 2])
        ve = sb("ve", [P, 4 * NT])
        rstd = sb("rstd", [P, 4 * NT])
        nbias = sb("nbias", [P, 4 * NT])
        mx = sb("mx", [P, NT])
        nmx = sb("nmx", [P, NT])
        den = sb("den", [P, NT])
        rden = sb("rden", [P, NT])
        cmx = sb("cmx", [P, TPB])
        csum = sb("csum", [P, TPB])
        crec = sb("crec", [P, TPB])
        qsel = sb("qsel", [P, 2, NT])

        t_bank = [ctx.enter_context(nc.psum_tensor(f"t_bank{i}", [P, 512], F32)) for i in range(T_BANKS)]
        m_bank = [ctx.enter_context(nc.psum_tensor(f"m_bank{i}", [P, 512], F32)) for i in range(M_BANKS)]

        ld = {k: sem("ld_" + k) for k in ("w2", "w1", "sparse", "x0", "x1", "x2", "x3", "ffn", "cen",
                                          "wqkv", "wo", "small", "bias")}
        consts = sem("consts")
        t_done = sem("t_done")
        t_hi = sem("t_hi")
        t_free = sem("t_free")
        m_done = sem("m_done")
        m_act = sem("m_act")
        m_dve = sem("m_dve")
        m_hi = sem("m_hi")
        stats_done = sem("stats_done")
        rstd_done = sem("rstd_done")
        norm_done = sem("norm_done")
        w1_hi_done = sem("w1_hi_done")
        w1_split = sem("w1_split")
        attn_hi_done = sem("attn_hi_done")
        attn_split = sem("attn_split")
        bias_split = sem("bias_split")
        late_split = sem("late_split")
        x1_done = sem("x1_done")
        x2_done = sem("x2_done")
        out_done = sem("out_done")
        bo_added = sem("bo_added")
        y_masked = sem("y_masked")
        max_done = sem("max_done")
        c_shift = sem("c_shift")
        c_exp = sem("c_exp")
        csel_done = sem("csel_done")
        best_done = sem("best_done")
        onehot_done = sem("onehot_done")
        chain = sem("chain")
        pchain = sem("pchain")
        stored = sem("stored")

        def m_freed(m):
            dve = M_JOBS[m][0] in FREED_BY_VECTOR
            n = sum((j[0] in FREED_BY_VECTOR) == dve for j in M_JOBS[:m + 1])
            return (m_dve if dve else m_act), n

        def feat(tensor, t):
            return tensor[:, :, t * P:(t + 1) * P]

        def clustered_in(b):
            return (odd_hi, odd_lo) if b == NB - 1 else (even_hi, even_lo)

        def f32(ap):
            return ap.bitcast(F32)

        def split_of(what, b, t):
            if what in ("x1", "x3"):
                return feat(odd_hi, t), feat(odd_lo, t)
            if what in ("x2", "x4"):
                hi, lo = clustered_in(b)
                return feat(hi, t), feat(lo, t)
            if what == "w2":
                return w2t_hi[:, t, :], w2t_lo[:, t, :]
            if what == "ffn":
                return ffn_hi[:, t, :], ffn_lo[:, t, :]
            if what == "cen":
                return cen_hl[:, :, 0:NC], cen_hl[:, :, NC:2 * NC]
            if what == "v":
                return v_hi, v_lo
            return feat(pt_hi, t), feat(pt_lo, t)

        def bank_view(what, bank):
            if what == "cen":
                return bank[:, 0:KC * NC].rearrange("p (k c) -> p k c", k=KC)
            if what in ("w2", "ffn", "v"):
                return bank[:, :]
            return bank[:, :].rearrange("p (k c) -> p k c", k=KC)

        block = ctx.enter_context(nc.Block())

        @block.sync
        def _(sp):
            rows_of = lambda d: d.rearrange("(c p) n -> p c n", p=P)

            def load_x(b):
                sp.dma_start(x_tok[:, b * TPB:(b + 1) * TPB, :], rows_of(x_d[b])).then_inc(ld[f"x{b}"], 16)

            sp.dma_start(w2_raw[:, :, :], rows_of(w2_d)).then_inc(ld["w2"], 16)
            sp.dma_start(w1_raw[:, :, :], rows_of(w1_d)).then_inc(ld["w1"], 16)
            load_x(0)
            sp.dma_start(sparse, rows_of(sparse_d)).then_inc(ld["sparse"], 16)
            sp.dma_start(cen_raw, cen_d).then_inc(ld["cen"], 16)
            sp.wait_ge(t_done, T_AT["w2", 0, KC - 1] + 1)
            sp.dma_start(ffn_raw[:, :, :], rows_of(ffn_d)).then_inc(ld["ffn"], 16)
            load_x(1)
            sp.wait_ge(attn_split, KC)
            sp.dma_start(wo_raw, wo_d).then_inc(ld["wo"], 16)
            sp.dma_start(wqkv_raw, rows_of(wqkv_d)).then_inc(ld["wqkv"], 16)
            load_x(2)
            load_x(3)
            outs = [b * TPB + t for kind, _, b, t in STEPS if kind == "out"]
            for at, n in enumerate(outs):
                sp.wait_ge(out_done, at + 1)
                sp.dma_start(out_d[n // TPB, (n % TPB) * P:(n % TPB + 1) * P, :], x_tok[:, n, :]).then_inc(stored, 16)
            sp.wait_ge(stored, 16 * NT)

        @block.gpsimd
        def _(pool):
            pchained = [0]

            def link(ins):
                pchained[0] += 1
                ins.then_inc(pchain, 1)
                pool.wait_ge(pchain, pchained[0])

            pool.memset(ident[:, :], 0.0).then_inc(pchain, 1)
            pchained[0] += 1
            pool.wait_ge(pchain, 1)
            pool.affine_select(out=ident[:, :], in_=ident[:, :], compare_op=ALU.not_equal, fill=1.0,
                               base=0, pattern=[[-1, P]], channel_multiplier=1).then_inc(consts, 1)
            pool.memset(half[:, :], -0.5).then_inc(consts, 1)
            pool.memset(f32(ones[:, :]), 1.0).then_inc(consts, 1)
            pool.memset(f32(bias1[:, :]), 0.0).then_inc(consts, 1)
            pool.memset(f32(bias2[:, :]), 0.0).then_inc(consts, 1)
            pool.memset(f32(csel[:, :]), 0.0).then_inc(consts, 1)
            pool.memset(best[:, :, :], 0.0).then_inc(consts, 1)
            pool.iota(cluster[:, :], pattern=[[0, 1]], base=0, channel_multiplier=1,
                      allow_small_or_imprecise_dtypes=True).then_inc(consts, 1)

            pieces = [("hi", c) for c in range(KC + 1)] + [("lo", c) for c in range(KC + 1)]

            def split_late(part, c):
                if (part, c) == ("hi", 0):
                    pool.wait_ge(ld["wqkv"], 16)
                    pool.wait_ge(ld["wo"], 16)
                if (part, c) == ("lo", 0):
                    pool.wait_ge(late_split, KC + 1)
                raw = wo_raw if c == KC else wqkv_raw[:, c, :]
                hi = wo_hi[:, :] if c == KC else wqkv_hi[:, c, :]
                lo = wo_lo[:, :] if c == KC else wqkv_lo[:, c, :]
                if part == "hi":
                    pool.tensor_copy(hi, raw).then_inc(late_split, 1)
                else:
                    pool.tensor_tensor(lo, raw, f32(hi), ALU.subtract).then_inc(late_split, 1)

            for kind, what, b, t in STEPS:
                n = b * TPB + t
                if kind == "stats":
                    at = STAT_AT[what, b, t]
                    i = (what - 1) * NT + n
                    pool.wait_ge(stats_done, at + 1)
                    link(pool.tensor_scalar(ve[:, i:i + 1], mv[:, i, 1:2], EPS, None, ALU.add))
                    link(pool.tensor_tensor(rstd[:, i:i + 1], ve[:, i:i + 1], half[:, :], ALU.pow))
                    pool.tensor_scalar(nbias[:, i:i + 1], mv[:, i, 0:1], rstd[:, i:i + 1], -1.0, ALU.mult,
                                       ALU.mult).then_inc(rstd_done, 1)
                    if (what == 2 and b >= 1 or what == 1 and b >= 2) and pieces:
                        split_late(*pieces.pop(0))
                elif (kind, what, b, t) in MASK_AT:
                    last = "mask2" if kind == "x2" else "mask4"
                    pool.wait_ge(*m_freed(M_AT[last, 0, 0]))
                    pool.wait_ge(*m_freed(M_AT["dn2" if kind == "x2" else "dn4", b, t]))
                    pool.tensor_tensor(y_tok[:, n, :], y_tok[:, n, :], rows[:, :], ALU.mult).then_inc(y_masked, 1)
                elif kind == "norm" and what == 3:
                    pool.wait_ge(norm_done, NORM_AT[3, b, t] + 1)
                    if n == 0:
                        pool.wait_ge(ld["bias"], 16)
                    pool.tensor_tensor(x_tok[:, n, :], x_tok[:, n, :], bo[:, :], ALU.add).then_inc(bo_added, 1)

        @block.scalar
        def _(act):
            act.dma_start(bias_raw[0:1, 0, :], b2_d.rearrange("(a n) -> a n", a=1)).then_inc(ld["small"], 16)
            act.dma_start(bias_raw[32:33, 0, :], b2_d.rearrange("(a n) -> a n", a=1)).then_inc(ld["small"], 16)
            act.dma_start(bias_raw[0:1, 1, :], fb_d.rearrange("(a n) -> a n", a=1)).then_inc(ld["small"], 16)
            act.dma_start(bias_raw[32:33, 1, :], fb_d.rearrange("(a n) -> a n", a=1)).then_inc(ld["small"], 16)
            act.dma_start(bqkv[:, :], bqkv_d.rearrange("(j p) -> p j", p=P),
                          allow_slow_non_contiguous=True).then_inc(ld["small"], 16)
            act.dma_start(assign, assign_d.rearrange("(a n) -> a n", a=1).broadcast_to([P, D])).then_inc(ld["small"], 16)
            act.dma_start(bo[:, :], bo_d.rearrange("(a n) -> a n", a=1).broadcast_to([P, D])).then_inc(ld["bias"], 16)

            for kind, what, b, t in STEPS:
                n = b * TPB + t
                if kind == "w1":
                    if t == 0:
                        act.wait_ge(ld["w1"], 16)
                    act.activation(w1_hi[:, t, :], w1_raw[:, t, :], ACT.Copy).then_inc(w1_hi_done, 1)
                elif kind == "norm":
                    i = (what - 1) * NT + n
                    dst = (xn_odd, xn_even)[(what - 1) % 2]
                    act.wait_ge(rstd_done, STAT_AT[what, b, t] + 1)
                    if b:
                        act.wait_ge(t_done, T_AT[f"x{what}", b - 1, t] + 1)
                    elif what >= 3:
                        act.wait_ge(t_done, T_AT[f"x{what - 2}", NB - 1, t] + 1)
                    act.activation(dst[:, t, :], x_tok[:, n, :], ACT.Identity, bias=nbias[:, i:i + 1],
                                   scale=rstd[:, i:i + 1]).then_inc(norm_done, 1)
                elif kind == "T" and (what, b, t) in HI_AT:
                    j = T_AT[what, b, t]
                    act.wait_ge(t_done, j + 1)
                    if what == "x1" and b >= 1:
                        act.wait_ge(m_done, M_AT["y1", b - 1, t] + 1)
                    elif what == "x2" and b == NB - 1:
                        act.wait_ge(m_done, M_AT["y1", b, t] + 1)
                    elif what == "x2":
                        act.wait_ge(m_done, (M_AT["dn2", b - 1, t] if b else M_AT["attn", 0, KC - 1]) + 1)
                    elif what == "x3":
                        act.wait_ge(m_done, (M_AT["v", b - 1, 0] if b else M_AT["dn2", NB - 1, t]) + 1)
                    elif what == "x4" and b == NB - 1:
                        act.wait_ge(m_done, M_AT["v", b, 0] + 1)
                    elif what == "x4":
                        act.wait_ge(m_done, (M_AT["dn4", b - 1, t] if b else M_AT["dn2", NB - 2, t]) + 1)
                    elif what in ("p", "v") and b >= 1:
                        act.wait_ge(m_done, M_AT["pv", b - 1, 0] + 1)
                    elif what in ("p", "v"):
                        act.wait_ge(m_done, M_AT["y1", NB - 1, TPB - 1] + 1)
                    act.activation(split_of(what, b, t)[0], bank_view(what, t_bank[j % T_BANKS]), ACT.Copy).then_inc(t_hi, 1)
                elif kind == "split_attn":
                    act.wait_ge(*m_freed(M_AT["attn", 0, t]))
                    act.activation(attn_hi[:, t, :], attn_f[:, t, :], ACT.Copy).then_inc(attn_hi_done, 1)
                elif kind == "M" and what != "attn" and what != "wo":
                    m = M_AT[what, b, t]
                    bank = m_bank[m % M_BANKS]
                    if what != "sc":
                        act.wait_ge(m_done, m + 1)
                    if what == "y1":
                        if n >= 2:
                            act.wait_ge(x1_done, n - 1)
                        act.activation(gelu[:, n % 2, :], bank[:, :], ACT.Gelu).then_inc(m_act, 1)
                    elif what in ("dn2", "dn4"):
                        if what == "dn4":
                            act.wait_ge(x2_done, n + 1)
                        elif n == 2 * KC:
                            act.wait_ge(late_split, 2 * KC + 2)
                        elif n == NT - 2:
                            act.wait_ge(x1_done, NT)
                        act.activation(y_tok[:, n, :], bank[:, :], ACT.Copy).then_inc(m_act, 1)
                    elif what in ("cl2", "cl4"):
                        first = "tc2" if b or what == "cl2" else "tc2"
                        if what == "cl2" and b:
                            act.wait_ge(t_done, T_AT["tc2", b - 1, 0] + 1)
                        if what == "cl4":
                            act.wait_ge(t_done, (T_AT["tc4", b - 1, 0] if b else T_AT["tc2", NB - 1, 0]) + 1)
                        act.activation(lg[:, :], bank[:, :], ACT.Copy).then_inc(m_act, 1)
                    elif what in ("q", "k"):
                        if b:
                            act.wait_ge(m_done, M_AT["sc", b - 1, TPB - 1] + 1)
                        j = "qk".index(what)
                        if b == 0 and what == "q":
                            act.wait_ge(ld["small"], 96)
                        act.activation((q_hi, k_hi)[j], bank[:, :], ACT.Identity,
                                       bias=bqkv[:, j:j + 1]).then_inc(m_hi, 1)
                    elif what == "v":
                        if b:
                            act.wait_ge(t_done, T_AT["v", b - 1, 0] + 1)
                        else:
                            act.wait_ge(late_split, 2 * KC + 2)
                        act.activation(vt[:, :], bank[:, :], ACT.Identity, bias=bqkv[:, 2:3]).then_inc(m_act, 1)
                    elif what == "pv":
                        if b:
                            act.wait_ge(m_done, M_AT["wo", b - 1, TPB - 1] + 1)
                        act.activation(o_hi, bank[:, :], ACT.Copy).then_inc(m_hi, 1)
                elif kind == "exp":
                    m = M_AT["sc", b, t]
                    act.wait_ge(max_done, n + 1)
                    if b:
                        act.wait_ge(t_done, T_AT["p", b - 1, t] + 1)
                    act.activation(p_tok[:, t, :], m_bank[m % M_BANKS][:, :], ACT.Exp, bias=nmx[:, n:n + 1],
                                   scale=SCALE, accum_out=den[:, n:n + 1]).then_inc(m_act, 1)
                elif kind in ("logit2", "logit4"):
                    act.wait_ge(c_shift, SOFT.index((kind[-1], b)) + 1)
                    act.activation(ce[:, :, :], cl[:, :, :], ACT.Exp, scale=INV_TEMPERATURE).then_inc(c_exp, 1)
                elif kind in ("mask2", "mask4"):
                    m = M_AT[kind, 0, 0]
                    act.wait_ge(m_done, m + 1)
                    if kind == "mask4":
                        act.wait_ge(y_masked, sum(s[0] == "x2" for s in MASK_AT))
                    act.activation(rows[:, :], m_bank[m % M_BANKS][:, :], ACT.Copy).then_inc(m_act, 1)

        @block.vector
        def _(dve):
            chained = [0]

            def link(ins):
                chained[0] += 1
                ins.then_inc(chain, 1)
                dve.wait_ge(chain, chained[0])

            for kind, what, b, t in STEPS:
                n = b * TPB + t
                if kind == "lo":
                    j = T_AT[what, b, t]
                    hi, lo = split_of(what, b, t)
                    dve.wait_ge(t_hi, HI_AT[what, b, t] + 1)
                    dve.tensor_tensor(lo, bank_view(what, t_bank[j % T_BANKS]), f32(hi), ALU.subtract).then_inc(t_free, 1)
                elif kind == "stats":
                    i = (what - 1) * NT + n
                    at = STAT_AT[what, b, t]
                    if what == 1:
                        dve.wait_ge(ld[f"x{b}"], 16)
                    elif what == 4:
                        dve.wait_ge(*m_freed(M_AT["wo", b, t]))
                    else:
                        dve.wait_ge((x1_done, x2_done)[what - 2], n + 1)
                    link(dve.bn_stats(st[:, at % 2, :], x_tok[:, n, :]))
                    dve.bn_aggr(mv[:, i, :], st[:, at % 2, :]).then_inc(stats_done, 1)
                elif kind == "w1":
                    dve.wait_ge(w1_hi_done, t + 1)
                    dve.tensor_tensor(w1_lo[:, t, :], w1_raw[:, t, :], f32(w1_hi[:, t, :]),
                                      ALU.subtract).then_inc(w1_split, 1)
                elif kind == "mask_attn":
                    m = M_AT["attn", 0, t]
                    if t == 0:
                        dve.wait_ge(ld["sparse"], 16)
                    dve.wait_ge(m_done, m + 1)
                    dve.tensor_tensor(attn_f[:, t, :], m_bank[m % M_BANKS][:, :], sparse[:, t, :],
                                      ALU.mult).then_inc(m_dve, 1)
                elif kind == "split_attn":
                    dve.wait_ge(attn_hi_done, t + 1)
                    dve.tensor_tensor(attn_lo[:, t, :], attn_f[:, t, :], f32(attn_hi[:, t, :]),
                                      ALU.subtract).then_inc(attn_split, 1)
                elif kind == "biases":
                    dve.wait_ge(ld["small"], 96)
                    dve.wait_ge(consts, 8)
                    for j, bias in enumerate((bias1, bias2)):
                        link(dve.tensor_copy(bias[0:1, :], bias_raw[0:1, j, :]))
                        link(dve.tensor_copy(bias[32:33, :], bias_raw[32:33, j, :]))
                        link(dve.tensor_tensor(bias[32:33, :], bias_raw[32:33, j, :], f32(bias[32:33, :]),
                                               ALU.subtract))
                    dve.tensor_scalar(onehot[:, :], assign, cluster[:, 0:1], None, ALU.is_equal)\
                       .then_inc(bias_split, 1)
                elif kind == "x1":
                    dve.wait_ge(*m_freed(M_AT["y1", b, t]))
                    dve.tensor_tensor(x_tok[:, n, :], x_tok[:, n, :], gelu[:, n % 2, :], ALU.add).then_inc(x1_done, 1)
                elif kind in ("x2", "out"):
                    late = kind == "out"
                    if masked_by_vector(kind, what, b, t):
                        dve.wait_ge(*m_freed(M_AT["mask4" if late else "mask2", 0, 0]))
                        dve.wait_ge(*m_freed(M_AT["dn4" if late else "dn2", b, t]))
                        link(dve.tensor_tensor(y_tok[:, n, :], y_tok[:, n, :], rows[:, :], ALU.mult))
                    else:
                        dve.wait_ge(y_masked, MASK_AT[kind, what, b, t] + 1)
                    dve.scalar_tensor_tensor(out=x_tok[:, n, :], in0=y_tok[:, n, :], scalar=qsel[:, int(late), n:n + 1],
                                             in1=x_tok[:, n, :], op0=ALU.mult, op1=ALU.add)\
                       .then_inc(out_done if late else x2_done, 1)
                elif kind in ("lo_q", "lo_k"):
                    c = ("lo_q", "lo_k").index(kind)
                    m = M_AT["qk"[c], b, 0]
                    hi, lo = ((q_hi, q_lo), (k_hi, k_lo))[c]
                    dve.wait_ge(m_hi, 3 * b + c + 1)
                    dve.scalar_tensor_tensor(out=lo, in0=m_bank[m % M_BANKS][:, :], scalar=bqkv[:, c:c + 1],
                                             in1=f32(hi), op0=ALU.add, op1=ALU.subtract).then_inc(m_dve, 1)
                elif kind == "lo_o":
                    m = M_AT["pv", b, 0]
                    dve.wait_ge(m_hi, 3 * b + 3)
                    dve.tensor_tensor(o_lo, m_bank[m % M_BANKS][:, :], f32(o_hi), ALU.subtract).then_inc(m_dve, 1)
                elif kind == "exp":
                    m = M_AT["sc", b, t]
                    dve.wait_ge(m_done, m + 1)
                    link(dve.tensor_reduce(out=mx[:, n:n + 1], in_=m_bank[m % M_BANKS][:, :], op=ALU.max, axis=AX.X))
                    dve.tensor_scalar(nmx[:, n:n + 1], mx[:, n:n + 1], -SCALE, None, ALU.mult).then_inc(max_done, 1)
                elif kind == "x3":
                    m = M_AT["wo", b, t]
                    dve.wait_ge(*m_freed(M_AT["sc", b, t]))
                    link(dve.reciprocal(rden[:, n:n + 1], den[:, n:n + 1]))
                    dve.wait_ge(m_done, m + 1)
                    dve.wait_ge(bo_added, n + 1)
                    dve.scalar_tensor_tensor(out=x_tok[:, n, :], in0=m_bank[m % M_BANKS][:, :],
                                             scalar=rden[:, n:n + 1], in1=x_tok[:, n, :],
                                             op0=ALU.mult, op1=ALU.add).then_inc(m_dve, 1)
                elif kind in ("logit2", "logit4"):
                    tc = T_AT["tc" + kind[-1], b, 0]
                    at = SOFT.index((kind[-1], b))
                    bank = t_bank[tc % T_BANKS][:, :].rearrange("p (t h c) -> p t c h", t=TPB, h=2)
                    dve.wait_ge(t_done, tc + 1)
                    if at:
                        dve.wait_ge(c_exp, at)
                    dve.tensor_reduce(out=cl[:, :, :], in_=bank, op=ALU.add, axis=AX.X).then_inc(t_free, 1)
                    dve.wait_ge(t_free, tc + 1)
                    link(dve.tensor_reduce(out=cmx[:, :], in_=cl[:, :, :], op=ALU.max, axis=AX.X))
                    dve.tensor_tensor(cl[:, :, :], cl[:, :, :], cmx[:, :].unsqueeze(2).broadcast_to([P, TPB, NC]),
                                      ALU.subtract).then_inc(c_shift, 1)
                elif kind in ("prob2", "prob4"):
                    at = SOFT.index((kind[-1], b))
                    late = kind == "prob4"
                    dve.wait_ge(c_exp, at + 1)
                    link(dve.tensor_reduce(out=csum[:, :], in_=ce[:, :, :], op=ALU.add, axis=AX.X))
                    link(dve.reciprocal(crec[:, :], csum[:, :]))
                    link(dve.tensor_tensor(cl[:, :, :], ce[:, :, :], crec[:, :].unsqueeze(2).broadcast_to([P, TPB, NC]),
                                           ALU.mult))
                    link(dve.tensor_reduce(out=cmx[:, :], in_=cl[:, :, :], op=ALU.max, axis=AX.X))
                    dve.tensor_scalar(qsel[:, int(late), b * TPB:(b + 1) * TPB], cmx[:, :], THRESHOLD, None, ALU.is_gt)
                    if late and b == 0:
                        link(dve.tensor_copy(best[:, :, :], cl[:, :, :]))
                    else:
                        link(dve.tensor_tensor(best[:, :, :], best[:, :, :], cl[:, :, :], ALU.max))
                elif kind in ("best2", "best4"):
                    tm = T_AT[kind, 0, 0]
                    dve.tensor_reduce(out=best1[:, :], in_=best[:, :, :].rearrange("p t c -> p c t"), op=ALU.max,
                                      axis=AX.X).then_inc(best_done, 1)
                    dve.wait_ge(t_done, tm + 1)
                    dve.tensor_reduce(out=csel1[:, :], in_=t_bank[tm % T_BANKS][0:NC, 0:P], op=ALU.max,
                                      axis=AX.X).then_inc(t_free, 1)
                    dve.wait_ge(t_free, tm + 1)
                    dve.tensor_scalar(csel[0:NC, :], csel1[:, :].broadcast_to([NC, P]), THRESHOLD, None,
                                      ALU.is_gt).then_inc(csel_done, 1)

        @block.tensor
        def _(pe):
            pe.wait_ge(consts, 8)

            def products(bank, pairs, bias=None):
                count = 3 * len(pairs) + (bias is not None)
                n = 0
                for (a_hi, a_lo), (w_hi, w_lo) in pairs:
                    for a, w in ((a_hi, w_hi), (a_lo, w_hi), (a_hi, w_lo)):
                        ins = pe.matmul(bank[:, :], a, w, start=(n == 0), stop=(n == count - 1))
                        n += 1
                if bias is not None:
                    ins = pe.matmul(bank[:, :], ones[:, :], bias[:, :], start=False, stop=True)
                return ins

            def t_free_for(j):
                if j >= T_BANKS:
                    pe.wait_ge(t_free, j - T_BANKS + 1)
                return t_bank[j % T_BANKS]

            def m_free_for(m):
                if m >= M_BANKS:
                    pe.wait_ge(*m_freed(m - M_BANKS))
                return m_bank[m % M_BANKS]

            def split_ready(what, b, t):
                pe.wait_ge(t_free, T_AT[what, b, t] + 1)

            for kind, what, b, t in STEPS:
                n = b * TPB + t
                if kind == "T":
                    j = T_AT[what, b, t]
                    bank = t_free_for(j)
                    if what in ("x1", "x2", "x3", "x4"):
                        stage = int(what[1])
                        src = (xn_odd, xn_even)[(stage - 1) % 2][:, t, :]
                        pe.wait_ge(norm_done, NORM_AT[stage, b, t] + 1)
                        blocks = [src[:, c * P:(c + 1) * P] for c in range(KC)]
                    elif what in ("w2", "ffn"):
                        raw = w2_raw if what == "w2" else ffn_raw
                        if t == 0:
                            pe.wait_ge(ld[what], 16)
                        blocks = [raw[:, c, t * P:(t + 1) * P] for c in range(KC)]
                    elif what == "cen":
                        pe.wait_ge(ld["cen"], 16)
                        blocks = [cen_raw[:, c * P:(c + 1) * P] for c in range(KC)]
                    elif what == "v":
                        pe.wait_ge(*m_freed(M_AT["v", b, 0]))
                        blocks = [vt[:, c * P:(c + 1) * P] for c in range(KC)]
                    elif what == "p":
                        pe.wait_ge(*m_freed(M_AT["sc", b, t]))
                        blocks = [p_tok[:, t, c * P:(c + 1) * P] for c in range(KC)]
                    else:
                        pe.wait_ge(*m_freed(M_AT["cl" + what[-1], b, 0]))
                        blocks = [lg[:, c * P:(c + 1) * P] for c in range(TPB)]
                    for c, blk in enumerate(blocks):
                        r = blk.shape[0]
                        ins = pe.transpose(bank[:, c * r:(c + 1) * r], blk, ident[0:r, 0:r])
                    ins.then_inc(t_done, 1)
                elif kind == "M":
                    m = M_AT[what, b, t]
                    bank = m_free_for(m)
                    cols = slice(t * P, (t + 1) * P)
                    if what == "attn":
                        if t == 0:
                            pe.wait_ge(w1_split, KC)
                            split_ready("w2", 0, KC - 1)
                        ins = products(bank, [((w1_hi[:, c, cols], w1_lo[:, c, cols]),
                                               (w2t_hi[:, c, :], w2t_lo[:, c, :])) for c in range(KC)])
                    elif what == "y1":
                        if b == 0 and t == 0:
                            pe.wait_ge(attn_split, KC)
                            pe.wait_ge(bias_split, 1)
                        split_ready("x1", b, t)
                        ins = products(bank, [((odd_hi[:, c, cols], odd_lo[:, c, cols]),
                                               (attn_hi[:, c, :], attn_lo[:, c, :])) for c in range(KC)], bias1)
                    elif what in ("cl2", "cl4"):
                        if what == "cl2" and b == 0:
                            split_ready("cen", 0, 0)
                        split_ready("x" + what[-1], b, TPB - 1)
                        for c in range(KC):
                            for h, a in enumerate(clustered_in(b)):
                                ins = pe.matmul(bank[:, :], cen_hl[:, c, :], a[:, c, :],
                                                start=(c + h == 0), stop=(c == KC - 1 and h == 1))
                    elif what in ("dn2", "dn4"):
                        if what == "dn2" and n == 0:
                            split_ready("ffn", 0, KC - 1)
                        hi, lo = clustered_in(b)
                        ins = products(bank, [((hi[:, c, cols], lo[:, c, cols]),
                                               (ffn_hi[:, c, :], ffn_lo[:, c, :])) for c in range(KC)], bias2)
                    elif what in ("q", "k", "v"):
                        w = slice("qkv".index(what) * DH, ("qkv".index(what) + 1) * DH)
                        if b == 0 and what == "q":
                            pe.wait_ge(late_split, 2 * KC + 2)
                        if what == "q":
                            split_ready("x3", b, TPB - 1)
                        ins = products(bank, [((wqkv_hi[:, c, w], wqkv_lo[:, c, w]),
                                               (odd_hi[:, c, :], odd_lo[:, c, :])) for c in range(KC)])
                    elif what == "sc":
                        if t == 0:
                            pe.wait_ge(*m_freed(M_AT["k", b, 0]))
                        ins = products(bank, [((q_hi[:, cols], q_lo[:, cols]), (k_hi, k_lo))])
                    elif what == "pv":
                        split_ready("v", b, 0)
                        split_ready("p", b, TPB - 1)
                        ins = products(bank, [((v_hi[:, c * P:(c + 1) * P], v_lo[:, c * P:(c + 1) * P]),
                                               (pt_hi[:, c, :], pt_lo[:, c, :])) for c in range(KC)])
                    elif what == "wo":
                        if t == 0:
                            pe.wait_ge(*m_freed(M_AT["pv", b, 0]))
                        ins = products(bank, [((o_hi[:, cols], o_lo[:, cols]), (wo_hi[:, :], wo_lo[:, :]))])
                    ins.then_inc(m_done, 1)
                elif kind in ("best2", "best4"):
                    j = T_AT[kind, 0, 0]
                    bank = t_free_for(j)
                    pe.wait_ge(best_done, 1 + (kind == "best4"))
                    pe.transpose(bank[0:NC, 0:P], best1[:, :], ident[:, :]).then_inc(t_done, 1)
                elif kind in ("mask2", "mask4"):
                    m = M_AT[kind, 0, 0]
                    bank = m_free_for(m)
                    pe.wait_ge(csel_done, 1 + (kind == "mask4"))
                    pe.matmul(bank[:, :], csel[:, :], onehot[:, :], start=True, stop=True).then_inc(m_done, 1)


_INS = ["L0_attn_a_x", "L0_attn_a_w1", "L0_attn_a_w2", "L0_attn_a_b2", "L0_attn_a_sparse_mask", "L0_attn_b_Wqkv",
        "L0_attn_b_bqkv", "L0_attn_b_Wo", "L0_attn_b_bo", "L0_ffn_weight", "L0_ffn_bias", "L0_ffn_centroids",
        "L0_ffn_assignments"]


def kernel(**inputs):
    import numpy as np
    import concourse.bacc as bacc
    from concourse.bass_utils import run_bass_kernel_spmd

    nc = bacc.Bacc("TRN2", target_bir_lowering=False, num_devices=1)
    arrays, args = {}, []
    for name in _INS:
        a = np.ascontiguousarray(inputs[name])
        arrays[f"in_{name}"] = a
        args.append(nc.dram_tensor(f"in_{name}", a.shape, mybir.dt.from_np(a.dtype), kind="ExternalInput").ap())
    out = nc.dram_tensor("out", (NB, S, D), F32, kind="ExternalOutput").ap()
    program(nc, *args, out)
    r = run_bass_kernel_spmd(nc, [arrays], core_ids=[0])
    return r.results[0]["out"]
```

```python
from contextlib import ExitStack

import concourse.bass as bass
from concourse import mybir

F32 = mybir.dt.float32
F32R = mybir.dt.float32r
I32 = mybir.dt.int32
ALU = mybir.AluOpType
ACT = mybir.ActivationFunctionType
AX = mybir.AxisListType

P = 128
NB, S, D = 4, 512, 512
TPB = S // P
NT = NB * TPB
KC = D // P
DH = D // 4
NC = 64
EPS = 1e-5
THRESHOLD = 0.01
INV_TEMPERATURE = 10.0
SCALE = float(DH) ** -0.5
T_BANKS = 4
M_BANKS = 4

FREED_BY_VECTOR = ("attn", "q", "k", "pv", "wo")


def schedule():
    o = []

    def step(*s):
        o.append(s)

    def transposed(what, b, t):
        step("T", what, b, t)
        step("lo", what, b, t)

    def residual(what, stage, b, t):
        step(what, "", b, t)
        step("stats", stage, b, t)

    for c in range(KC):
        step("T", "w2", 0, c)
        step("w1", "", 0, c)
        step("lo", "w2", 0, c)
    for t in range(TPB):
        step("M", "attn", 0, t)
        step("mask_attn", "", 0, t)
        if t:
            step("split_attn", "", 0, t - 1)
            step("norm", 1, 0, t - 1)
        step("stats", 1, 0, t)
    step("biases", "", 0, 0)
    step("T", "x1", 0, 0)
    step("split_attn", "", 0, TPB - 1)
    step("norm", 1, 0, TPB - 1)
    step("lo", "x1", 0, 0)
    for t in range(1, TPB):
        transposed("x1", 0, t)
    step("onehot", "", 0, 0)
    for t in range(TPB):
        step("T", "ffn", 0, t)
        if t >= 2:
            step("T", "x1", 1, t - 2)
        step("M", "y1", 0, t)
        if t:
            residual("x1", 2, 0, t - 1)
        step("lo", "ffn", 0, t)
        if t >= 2:
            step("lo", "x1", 1, t - 2)
        step("stats", 1, 1, t)
        if t:
            step("norm", 1, 1, t - 1)
            if t >= 2:
                step("norm", 2, 0, t - 2)
    transposed("cen", 0, 0)

    for b in range(1, NB):
        for t in range(TPB):
            jobs = []
            if b == 1 and t < 2:
                jobs.append(("x1", 1, t + 2))
            if b == 1 or t + 1 < TPB:
                jobs.append(("x2", b - 1, t + (b > 1)))
            for job in jobs:
                step("T", *job)
            step("M", "y1", b, t)
            if t:
                residual("x1", 2, b, t - 1)
            elif b == 1:
                residual("x1", 2, 0, TPB - 1)
            for job in jobs:
                step("lo", *job)
            if b == 1 and t == 0:
                step("norm", 1, 1, TPB - 1)
                step("norm", 2, 0, TPB - 2)
            elif b == 1 and t == 1:
                step("norm", 2, 0, TPB - 1)
            elif t >= 2:
                step("norm", 2, b, t - 2)
            if b + 1 < NB:
                step("stats", 1, b + 1, t)
                if t:
                    step("norm", 1, b + 1, t - 1)
        step("M", "cl2", b - 1, 0)
        residual("x1", 2, b, TPB - 1)
        step("norm", 2, b, TPB - 2)
        if b + 1 < NB:
            step("norm", 1, b + 1, TPB - 1)
            for t in range(TPB):
                step("T", "x1", b + 1, t)
                if t == TPB - 1:
                    step("T", "x2", b, 0)
                step("M", "dn2", b - 1, t)
                if t == 0:
                    step("norm", 2, b, TPB - 1)
                step("lo", "x1", b + 1, t)
                if t == TPB - 1:
                    step("lo", "x2", b, 0)
                if t == 0:
                    step("T", "tc2", b - 1, 0)
                    step("logit2", "", b - 1, 0)
                if t == 2:
                    step("prob2", "", b - 1, 0)
    clustered(step, transposed, 2)
    for t in range(TPB):
        step("masked", "x2", 0, t)
        if t:
            residual("x2", 3, 0, t - 1)
        if t >= 2:
            step("norm", 3, 0, t - 2)
            step("T", "x3", 0, t - 2)
        if t >= 3:
            step("lo", "x3", 0, t - 3)
    residual("x2", 3, 0, TPB - 1)
    step("norm", 3, 0, TPB - 2)
    step("T", "x3", 0, TPB - 2)
    step("norm", 3, 0, TPB - 1)
    step("lo", "x3", 0, TPB - 3)
    step("T", "x3", 0, TPB - 1)
    step("lo", "x3", 0, TPB - 2)
    step("lo", "x3", 0, TPB - 1)

    for b in range(NB):
        step("M", "q", b, 0)
        if b:
            residual("x3", 4, b - 1, TPB - 1)
            step("norm", 4, b - 1, TPB - 2)
            transposed("x4", b - 1, 0)
        step("M", "k", b, 0)
        step("lo_q", "", b, 0)
        if b:
            step("norm", 4, b - 1, TPB - 1)
            transposed("x4", b - 1, 1)
        step("M", "v", b, 0)
        step("lo_k", "", b, 0)
        if b + 1 < NB:
            for t in range(TPB):
                step("bias_o", "", b, t)
                step("masked", "x2", b + 1, t)
        else:
            for t in range(TPB):
                step("bias_o", "", b, t)
        if b:
            transposed("x4", b - 1, 2)
            transposed("x4", b - 1, 3)
        step("T", "v", b, 0)
        for t in range(TPB):
            step("M", "sc", b, t)
            step("exp", "", b, t)
            if t == 0:
                step("lo", "v", b, 0)
        fill = [("dn4", b - 1, t) for t in range(TPB)] if b else [("dn2", NB - 2, 2), ("dn2", NB - 2, 3)]
        if b == NB - 1:
            fill = fill[:1]
        if b:
            step("M", "cl4", b - 1, 0)
        if b + 1 < NB:
            residual("x2", 3, b + 1, 0)
        for t in range(TPB):
            step("T", "p", b, t)
            if b + 1 < NB and t >= 2:
                step("T", "x3", b + 1, t - 2)
            if fill and t < TPB - 1:
                step("M", *fill.pop(0))
            step("lo", "p", b, t)
            if b + 1 < NB:
                if t >= 2:
                    step("lo", "x3", b + 1, t - 2)
                if t:
                    step("norm", 3, b + 1, t - 1)
                if t % 2 == 0:
                    residual("x2", 3, b + 1, t // 2 + 1)
            if b and t == 0:
                step("T", "tc4", b - 1, 0)
                step("logit4", "", b - 1, 0)
        step("M", "pv", b, 0)
        if b + 1 < NB:
            residual("x2", 3, b + 1, TPB - 1)
            step("T", "x3", b + 1, TPB - 2)
            step("norm", 3, b + 1, TPB - 1)
            if fill:
                step("M", *fill.pop(0))
        step("lo_o", "", b, 0)
        if b + 1 < NB:
            step("lo", "x3", b + 1, TPB - 2)
        if b + 1 < NB:
            step("T", "x3", b + 1, TPB - 1)
        if b:
            step("prob4", "", b - 1, 0)
        for t in range(TPB):
            step("M", "wo", b, t)
        if b + 1 < NB:
            step("lo", "x3", b + 1, TPB - 1)
        for t in range(TPB - 1):
            residual("x3", 4, b, t)
            if t:
                step("norm", 4, b, t - 1)
    step("M", "dn4", NB - 2, 1)
    residual("x3", 4, NB - 1, TPB - 1)
    step("norm", 4, NB - 1, TPB - 2)
    clustered(step, transposed, 4)
    outs = [divmod(n if n < NT - 2 * TPB else n + TPB if n < NT - TPB else n - TPB, TPB) for n in range(NT)]
    for out in outs:
        step("masked", "out", *out)
        step("out", "", *out)
    return o


def clustered(step, transposed, stage):
    b, what = NB - 1, f"x{stage}"
    dense, clusters = f"dn{stage}", f"cl{stage}"
    for t in range(TPB):
        if t < 2 and stage == 2:
            step("M", dense, b - 1, t)
        if t == 0:
            step("norm", stage, b, TPB - 1)
        transposed(what, b, t)
        if stage == 2 and t == 0:
            step("T", "tc2", b - 1, 0)
            step("logit2", "", b - 1, 0)
    if stage == 2:
        step("prob2", "", b - 1, 0)
    step("M", clusters, b, 0)
    step("T", f"tc{stage}", b, 0)
    step("M", dense, b, 0)
    step(f"logit{stage}", "", b, 0)
    step("M", dense, b, 1)
    step(f"prob{stage}", "", b, 0)
    step(f"best{stage}", "", 0, 0)
    step("M", dense, b, 2)
    step(f"mask{stage}", "", 0, 0)
    step("M", dense, b, 3)
    if stage == 4:
        step("M", dense, b - 1, 2)
        step("M", dense, b - 1, 3)


def masked_by_vector(kind, b, t):
    return b * TPB + t < TPB and t % 2 == 0 if kind == "x2" else t % TPB == 2


def program(nc, x_d, w1_d, w2_d, b2_d, sparse_d, wqkv_d, bqkv_d, wo_d, bo_d, ffn_d, fb_d, cen_d,
            assign_d, out_d):
    STEPS = schedule()
    T_AT = {}
    M_AT = {}
    for s in STEPS:
        if s[0] == "T":
            T_AT[s[1:]] = len(T_AT)
        if s[0] in ("best2", "best4"):
            T_AT[s[0], 0, 0] = len(T_AT)
        if s[0] in ("mask2", "mask4"):
            M_AT[s[0], 0, 0] = len(M_AT)
        if s[0] == "M":
            M_AT[s[1:]] = len(M_AT)
    M_JOBS = list(M_AT)
    STAT_AT = {s[1:]: n for n, s in enumerate([s for s in STEPS if s[0] == "stats"])}
    MASK_AT = {s[1:]: n for n, s in enumerate([s for s in STEPS if s[0] == "masked" and not masked_by_vector(*s[1:])])}
    BIAS_AT = {s[2:]: n for n, s in enumerate([s for s in STEPS if s[0] == "bias_o"])}
    NORM_AT = {s[1:]: n for n, s in enumerate([s for s in STEPS if s[0] == "norm"])}
    HI_JOBS = [j for j in T_AT if j[0] not in ("tc2", "tc4", "best2", "best4")]
    HI_AT = {j: n for n, j in enumerate(HI_JOBS)}
    SOFT = [(s[0][-1], s[2]) for s in STEPS if s[0] in ("logit2", "logit4")]

    assert list(T_AT.values()) == [T_AT[j] for j in [
        (s[1:] if s[0] == "lo" else ("tc" + s[0][-1], s[2], 0) if s[0] in ("logit2", "logit4") else (s[0], 0, 0))
        for s in STEPS if s[0] in ("lo", "logit2", "logit4", "best2", "best4")]]

    ctx = ExitStack()
    with ctx:
        def sb(name, shape, dt=F32):
            return ctx.enter_context(nc.sbuf_tensor(name, shape, dt))

        def sem(name):
            return ctx.enter_context(nc.semaphore(name))

        x_tok = sb("x_tok", [P, NT, D])
        y_tok = sb("y_tok", [P, NT, D])
        odd_hi = sb("odd_hi", [P, KC, S], F32R)
        odd_lo = sb("odd_lo", [P, KC, S], F32R)
        even_hi = sb("even_hi", [P, KC, S], F32R)
        even_lo = sb("even_lo", [P, KC, S], F32R)
        xn_odd = sb("xn_odd", [P, TPB, D])
        xn_even = sb("xn_even", [P, TPB, D])
        w2_raw = sb("w2_raw", [P, KC, D])
        w1_raw = y_tok[:, KC:2 * KC, :]
        ffn_raw = w2_raw
        w1_hi, w1_lo = even_hi, even_lo
        w2t_hi = sb("w2t_hi", [P, KC, D], F32R)
        w2t_lo = sb("w2t_lo", [P, KC, D], F32R)
        pt_hi, pt_lo = w2t_hi, w2t_lo
        sparse = y_tok[:, NT - 2 * KC:NT - KC, :]
        attn_f = y_tok[:, NT - KC:NT, :]
        attn_hi = sb("attn_hi", [P, KC, D], F32R)
        attn_lo = sb("attn_lo", [P, KC, D], F32R)
        ffn_hi = sb("ffn_hi", [P, KC, D], F32R)
        ffn_lo = sb("ffn_lo", [P, KC, D], F32R)
        cen_hl = sb("cen_hl", [P, KC, 2 * NC], F32R)
        wqkv_raw = y_tok[:, 2 * KC:3 * KC, 0:3 * DH]
        wo_raw = y_tok[:, NT - 3, :]
        wqkv_hi = sb("wqkv_hi", [P, KC, 3 * DH], F32R)
        wqkv_lo = sb("wqkv_lo", [P, KC, 3 * DH], F32R)
        wo_hi = sb("wo_hi", [P, D], F32R)
        wo_lo = sb("wo_lo", [P, D], F32R)
        p_tok = w2_raw
        gelu = y_tok[:, NT - 2:NT, :]
        q_hi = attn_hi[:, 0, :]
        q_lo = attn_hi[:, 1, :]
        k_hi = attn_hi[:, 2, :]
        k_lo = attn_hi[:, 3, :]
        v_hi = attn_lo[:, 0, :]
        v_lo = attn_lo[:, 1, :]
        o_hi = attn_lo[:, 2, :]
        o_lo = attn_lo[:, 3, :]
        vt = sb("vt", [P, S])
        lg = sb("lg", [P, S])
        cen_raw = lg[0:NC, :]
        cl = sb("cl", [P, TPB, NC])
        ce = sb("ce", [P, TPB, NC])
        best = sb("best", [P, TPB, NC])
        best1 = sb("best1", [P, NC])
        onehot = sb("onehot", [P, D], F32R)
        assign = y_tok[:, 2, :].bitcast(I32)
        cluster = sb("cluster", [P, 1])
        csel = sb("csel", [P, P], F32R)
        csel1 = sb("csel1", [NC, 1])
        rows = sb("rows", [P, D])
        ident = sb("ident", [P, P])
        ones = sb("ones", [P, P], F32R)
        bias1 = sb("bias1", [P, D], F32R)
        bias2 = sb("bias2", [P, D], F32R)
        bias_raw = y_tok[0:33, 0:2, :]
        bqkv = sb("bqkv", [P, 3])
        bo = sb("bo", [P, D])
        half = sb("half", [P, 1])
        st = sb("st", [P, 2, 6])
        mv = sb("mv", [P, 4 * NT, 2])
        ve = sb("ve", [P, 4 * NT])
        rstd = sb("rstd", [P, 4 * NT])
        nbias = sb("nbias", [P, 4 * NT])
        mx = sb("mx", [P, NT])
        nmx = sb("nmx", [P, NT])
        den = sb("den", [P, NT])
        rden = sb("rden", [P, NT])
        cmx = sb("cmx", [P, TPB])
        csum = sb("csum", [P, TPB])
        crec = sb("crec", [P, TPB])
        qsel = sb("qsel", [P, 2, NT])

        t_bank = [ctx.enter_context(nc.psum_tensor(f"t_bank{i}", [P, 512], F32)) for i in range(T_BANKS)]
        m_bank = [ctx.enter_context(nc.psum_tensor(f"m_bank{i}", [P, 512], F32)) for i in range(M_BANKS)]

        ld = {k: sem("ld_" + k) for k in ("w2", "w1", "sparse", "x0", "x1", "x2", "x3", "ffn", "cen",
                                          "wqkv", "wo", "small", "bias")}
        consts = sem("consts")
        t_done = sem("t_done")
        t_hi = sem("t_hi")
        t_free = sem("t_free")
        m_done = sem("m_done")
        m_act = sem("m_act")
        m_dve = sem("m_dve")
        m_hi = sem("m_hi")
        stats_done = sem("stats_done")
        rstd_done = sem("rstd_done")
        norm_done = sem("norm_done")
        w1_hi_done = sem("w1_hi_done")
        w1_split = sem("w1_split")
        attn_hi_done = sem("attn_hi_done")
        attn_split = sem("attn_split")
        bias_split = sem("bias_split")
        late_split = sem("late_split")
        x1_done = sem("x1_done")
        x2_done = sem("x2_done")
        out_done = sem("out_done")
        bo_added = sem("bo_added")
        y_masked = sem("y_masked")
        max_done = sem("max_done")
        c_shift = sem("c_shift")
        c_exp = sem("c_exp")
        csel_done = sem("csel_done")
        best_done = sem("best_done")
        onehot_done = sem("onehot_done")
        chain = sem("chain")
        pchain = sem("pchain")
        stored = sem("stored")

        def m_freed(m):
            dve = M_JOBS[m][0] in FREED_BY_VECTOR
            n = sum((j[0] in FREED_BY_VECTOR) == dve for j in M_JOBS[:m + 1])
            return (m_dve if dve else m_act), n

        def feat(tensor, t):
            return tensor[:, :, t * P:(t + 1) * P]

        def clustered_in(b):
            return (odd_hi, odd_lo) if b == NB - 1 else (even_hi, even_lo)

        def f32(ap):
            return ap.bitcast(F32)

        def split_of(what, b, t):
            if what in ("x1", "x3"):
                return feat(odd_hi, t), feat(odd_lo, t)
            if what in ("x2", "x4"):
                hi, lo = clustered_in(b)
                return feat(hi, t), feat(lo, t)
            if what == "w2":
                return w2t_hi[:, t, :], w2t_lo[:, t, :]
            if what == "ffn":
                return ffn_hi[:, t, :], ffn_lo[:, t, :]
            if what == "cen":
                return cen_hl[:, :, 0:NC], cen_hl[:, :, NC:2 * NC]
            if what == "v":
                return v_hi, v_lo
            return feat(pt_hi, t), feat(pt_lo, t)

        def bank_view(what, bank):
            if what == "cen":
                return bank[:, 0:KC * NC].rearrange("p (k c) -> p k c", k=KC)
            if what in ("w2", "ffn", "v"):
                return bank[:, :]
            return bank[:, :].rearrange("p (k c) -> p k c", k=KC)

        block = ctx.enter_context(nc.Block())

        @block.sync
        def _(sp):
            rows_of = lambda d: d.rearrange("(c p) n -> p c n", p=P)

            def load_x(b):
                sp.dma_start(x_tok[:, b * TPB:(b + 1) * TPB, :], rows_of(x_d[b])).then_inc(ld[f"x{b}"], 16)

            sp.dma_start(w2_raw[:, :, :], rows_of(w2_d)).then_inc(ld["w2"], 16)
            sp.dma_start(w1_raw[:, :, :], rows_of(w1_d)).then_inc(ld["w1"], 16)
            load_x(0)
            sp.dma_start(sparse, rows_of(sparse_d)).then_inc(ld["sparse"], 16)
            sp.dma_start(cen_raw, cen_d).then_inc(ld["cen"], 16)
            sp.wait_ge(t_done, T_AT["w2", 0, KC - 1] + 1)
            sp.dma_start(ffn_raw[:, :, :], rows_of(ffn_d)).then_inc(ld["ffn"], 16)
            load_x(1)
            sp.wait_ge(attn_split, KC)
            sp.dma_start(wo_raw, wo_d).then_inc(ld["wo"], 16)
            sp.dma_start(wqkv_raw, rows_of(wqkv_d)).then_inc(ld["wqkv"], 16)
            load_x(2)
            load_x(3)
            outs = [b * TPB + t for kind, _, b, t in STEPS if kind == "out"]
            for at, n in enumerate(outs):
                sp.wait_ge(out_done, at + 1)
                sp.dma_start(out_d[n // TPB, (n % TPB) * P:(n % TPB + 1) * P, :], x_tok[:, n, :]).then_inc(stored, 16)
            sp.wait_ge(stored, 16 * NT)

        @block.gpsimd
        def _(pool):
            pchained = [0]

            def link(ins):
                pchained[0] += 1
                ins.then_inc(pchain, 1)
                pool.wait_ge(pchain, pchained[0])

            pool.memset(ident[:, :], 0.0).then_inc(pchain, 1)
            pchained[0] += 1
            pool.wait_ge(pchain, 1)
            pool.affine_select(out=ident[:, :], in_=ident[:, :], compare_op=ALU.not_equal, fill=1.0,
                               base=0, pattern=[[-1, P]], channel_multiplier=1).then_inc(consts, 1)
            pool.memset(half[:, :], -0.5).then_inc(consts, 1)
            pool.memset(f32(ones[:, :]), 1.0).then_inc(consts, 1)
            pool.memset(f32(bias1[:, :]), 0.0).then_inc(consts, 1)
            pool.memset(f32(bias2[:, :]), 0.0).then_inc(consts, 1)
            pool.memset(f32(csel[:, :]), 0.0).then_inc(consts, 1)
            pool.memset(best[:, :, :], 0.0).then_inc(consts, 1)
            pool.iota(cluster[:, :], pattern=[[0, 1]], base=0, channel_multiplier=1,
                      allow_small_or_imprecise_dtypes=True).then_inc(consts, 1)

            pieces = [("hi", c) for c in range(KC + 1)] + [("lo", c) for c in range(KC + 1)]

            def split_late(part, c):
                if (part, c) == ("hi", 0):
                    pool.wait_ge(ld["wqkv"], 16)
                    pool.wait_ge(ld["wo"], 16)
                if (part, c) == ("lo", 0):
                    pool.wait_ge(late_split, KC + 1)
                raw = wo_raw if c == KC else wqkv_raw[:, c, :]
                hi = wo_hi[:, :] if c == KC else wqkv_hi[:, c, :]
                lo = wo_lo[:, :] if c == KC else wqkv_lo[:, c, :]
                if part == "hi":
                    pool.tensor_copy(hi, raw).then_inc(late_split, 1)
                else:
                    pool.tensor_tensor(lo, raw, f32(hi), ALU.subtract).then_inc(late_split, 1)

            for kind, what, b, t in STEPS:
                n = b * TPB + t
                if kind == "stats":
                    at = STAT_AT[what, b, t]
                    i = (what - 1) * NT + n
                    pool.wait_ge(stats_done, at + 1)
                    link(pool.tensor_scalar(ve[:, i:i + 1], mv[:, i, 1:2], EPS, None, ALU.add))
                    link(pool.tensor_tensor(rstd[:, i:i + 1], ve[:, i:i + 1], half[:, :], ALU.pow))
                    pool.tensor_scalar(nbias[:, i:i + 1], mv[:, i, 0:1], rstd[:, i:i + 1], -1.0, ALU.mult,
                                       ALU.mult).then_inc(rstd_done, 1)
                    if (what == 2 and b >= 1 or what == 1 and b >= 2) and pieces:
                        split_late(*pieces.pop(0))
                elif kind == "biases":
                    pool.wait_ge(ld["small"], 96)
                    pool.wait_ge(consts, 8)
                    pool.wait_ge(rstd_done, TPB)
                    for j, bias in enumerate((bias1, bias2)):
                        link(pool.tensor_copy(bias[32:33, :], bias_raw[32:33, j, :]))
                        link(pool.tensor_copy(bias[0:1, :], bias_raw[0:1, j, :]))
                        pool.tensor_tensor(bias[32:33, :], bias_raw[32:33, j, :], f32(bias[32:33, :]),
                                           ALU.subtract).then_inc(bias_split, 1)
                        pool.wait_ge(bias_split, j + 1)
                elif kind == "masked" and (what, b, t) in MASK_AT:
                    last = "mask2" if what == "x2" else "mask4"
                    pool.wait_ge(*m_freed(M_AT[last, 0, 0]))
                    pool.wait_ge(*m_freed(M_AT["dn2" if what == "x2" else "dn4", b, t]))
                    pool.tensor_tensor(y_tok[:, n, :], y_tok[:, n, :], rows[:, :], ALU.mult).then_inc(y_masked, 1)
                elif kind == "bias_o":
                    pool.wait_ge(norm_done, NORM_AT[3, b, t] + 1)
                    if n == 0:
                        pool.wait_ge(ld["bias"], 16)
                    pool.tensor_tensor(x_tok[:, n, :], x_tok[:, n, :], bo[:, :], ALU.add).then_inc(bo_added, 1)

        @block.scalar
        def _(act):
            act.dma_start(bias_raw[0:1, 0, :], b2_d.rearrange("(a n) -> a n", a=1)).then_inc(ld["small"], 16)
            act.dma_start(bias_raw[32:33, 0, :], b2_d.rearrange("(a n) -> a n", a=1)).then_inc(ld["small"], 16)
            act.dma_start(bias_raw[0:1, 1, :], fb_d.rearrange("(a n) -> a n", a=1)).then_inc(ld["small"], 16)
            act.dma_start(bias_raw[32:33, 1, :], fb_d.rearrange("(a n) -> a n", a=1)).then_inc(ld["small"], 16)
            act.dma_start(bqkv[:, :], bqkv_d.rearrange("(j p) -> p j", p=P),
                          allow_slow_non_contiguous=True).then_inc(ld["small"], 16)
            act.dma_start(assign, assign_d.rearrange("(a n) -> a n", a=1).broadcast_to([P, D])).then_inc(ld["small"], 16)
            act.dma_start(bo[:, :], bo_d.rearrange("(a n) -> a n", a=1).broadcast_to([P, D])).then_inc(ld["bias"], 16)

            for kind, what, b, t in STEPS:
                n = b * TPB + t
                if kind == "w1":
                    if t == 0:
                        act.wait_ge(ld["w1"], 16)
                    act.activation(w1_hi[:, t, :], w1_raw[:, t, :], ACT.Copy).then_inc(w1_hi_done, 1)
                elif kind == "norm":
                    i = (what - 1) * NT + n
                    dst = (xn_odd, xn_even)[(what - 1) % 2]
                    act.wait_ge(rstd_done, STAT_AT[what, b, t] + 1)
                    if b:
                        act.wait_ge(t_done, T_AT[f"x{what}", b - 1, t] + 1)
                    elif what >= 3:
                        act.wait_ge(t_done, T_AT[f"x{what - 2}", NB - 1, t] + 1)
                    act.activation(dst[:, t, :], x_tok[:, n, :], ACT.Identity, bias=nbias[:, i:i + 1],
                                   scale=rstd[:, i:i + 1]).then_inc(norm_done, 1)
                elif kind == "T" and (what, b, t) in HI_AT:
                    j = T_AT[what, b, t]
                    act.wait_ge(t_done, j + 1)
                    if what == "x1" and b >= 1:
                        act.wait_ge(m_done, M_AT["y1", b - 1, t] + 1)
                    elif what == "x2" and b == NB - 1:
                        act.wait_ge(m_done, M_AT["y1", b, t] + 1)
                    elif what == "x2":
                        act.wait_ge(m_done, (M_AT["dn2", b - 1, t] if b else M_AT["attn", 0, KC - 1]) + 1)
                    elif what == "x3":
                        act.wait_ge(m_done, (M_AT["v", b - 1, 0] if b else M_AT["dn2", NB - 1, t]) + 1)
                    elif what == "x4" and b == NB - 1:
                        act.wait_ge(m_done, M_AT["v", b, 0] + 1)
                    elif what == "x4":
                        act.wait_ge(m_done, (M_AT["dn4", b - 1, t] if b else M_AT["dn2", NB - 2, t]) + 1)
                    elif what in ("p", "v") and b >= 1:
                        act.wait_ge(m_done, M_AT["pv", b - 1, 0] + 1)
                    elif what in ("p", "v"):
                        act.wait_ge(m_done, M_AT["y1", NB - 1, TPB - 1] + 1)
                    act.activation(split_of(what, b, t)[0], bank_view(what, t_bank[j % T_BANKS]), ACT.Copy).then_inc(t_hi, 1)
                elif kind == "split_attn":
                    act.wait_ge(*m_freed(M_AT["attn", 0, t]))
                    act.activation(attn_hi[:, t, :], attn_f[:, t, :], ACT.Copy).then_inc(attn_hi_done, 1)
                elif kind == "M" and what != "attn" and what != "wo":
                    m = M_AT[what, b, t]
                    bank = m_bank[m % M_BANKS]
                    if what != "sc":
                        act.wait_ge(m_done, m + 1)
                    if what == "y1":
                        if n >= 2:
                            act.wait_ge(x1_done, n - 1)
                        act.activation(gelu[:, n % 2, :], bank[:, :], ACT.Gelu).then_inc(m_act, 1)
                    elif what in ("dn2", "dn4"):
                        if what == "dn4":
                            act.wait_ge(x2_done, n + 1)
                        elif n == 2 * KC:
                            act.wait_ge(late_split, 2 * KC + 2)
                        elif n == NT - 2:
                            act.wait_ge(x1_done, NT)
                        act.activation(y_tok[:, n, :], bank[:, :], ACT.Copy).then_inc(m_act, 1)
                    elif what in ("cl2", "cl4"):
                        first = "tc2" if b or what == "cl2" else "tc2"
                        if what == "cl2" and b:
                            act.wait_ge(t_done, T_AT["tc2", b - 1, 0] + 1)
                        if what == "cl4":
                            act.wait_ge(t_done, (T_AT["tc4", b - 1, 0] if b else T_AT["tc2", NB - 1, 0]) + 1)
                        act.activation(lg[:, :], bank[:, :], ACT.Copy).then_inc(m_act, 1)
                    elif what in ("q", "k"):
                        if b:
                            act.wait_ge(m_done, M_AT["sc", b - 1, TPB - 1] + 1)
                        j = "qk".index(what)
                        if b == 0 and what == "q":
                            act.wait_ge(ld["small"], 96)
                        act.activation((q_hi, k_hi)[j], bank[:, :], ACT.Identity,
                                       bias=bqkv[:, j:j + 1]).then_inc(m_hi, 1)
                    elif what == "v":
                        if b:
                            act.wait_ge(t_done, T_AT["v", b - 1, 0] + 1)
                        else:
                            act.wait_ge(late_split, 2 * KC + 2)
                        act.activation(vt[:, :], bank[:, :], ACT.Identity, bias=bqkv[:, 2:3]).then_inc(m_act, 1)
                    elif what == "pv":
                        if b:
                            act.wait_ge(m_done, M_AT["wo", b - 1, TPB - 1] + 1)
                        act.activation(o_hi, bank[:, :], ACT.Copy).then_inc(m_hi, 1)
                elif kind == "exp":
                    m = M_AT["sc", b, t]
                    act.wait_ge(max_done, n + 1)
                    if b:
                        act.wait_ge(t_done, T_AT["p", b - 1, t] + 1)
                    act.activation(p_tok[:, t, :], m_bank[m % M_BANKS][:, :], ACT.Exp, bias=nmx[:, n:n + 1],
                                   scale=SCALE, accum_out=den[:, n:n + 1]).then_inc(m_act, 1)
                elif kind in ("logit2", "logit4"):
                    act.wait_ge(c_shift, SOFT.index((kind[-1], b)) + 1)
                    act.activation(ce[:, :, :], cl[:, :, :], ACT.Exp, scale=INV_TEMPERATURE).then_inc(c_exp, 1)
                elif kind in ("mask2", "mask4"):
                    m = M_AT[kind, 0, 0]
                    act.wait_ge(m_done, m + 1)
                    if kind == "mask4":
                        act.wait_ge(y_masked, sum(s[0] == "x2" for s in MASK_AT))
                        act.wait_ge(x2_done, NT)
                    act.activation(rows[:, :], m_bank[m % M_BANKS][:, :], ACT.Copy).then_inc(m_act, 1)

        @block.vector
        def _(dve):
            chained = [0]

            def link(ins):
                chained[0] += 1
                ins.then_inc(chain, 1)
                dve.wait_ge(chain, chained[0])

            for kind, what, b, t in STEPS:
                n = b * TPB + t
                if kind == "lo":
                    j = T_AT[what, b, t]
                    hi, lo = split_of(what, b, t)
                    dve.wait_ge(t_hi, HI_AT[what, b, t] + 1)
                    dve.tensor_tensor(lo, bank_view(what, t_bank[j % T_BANKS]), f32(hi), ALU.subtract).then_inc(t_free, 1)
                elif kind == "stats":
                    i = (what - 1) * NT + n
                    at = STAT_AT[what, b, t]
                    if what == 1:
                        dve.wait_ge(ld[f"x{b}"], 16)
                    elif what == 4:
                        dve.wait_ge(*m_freed(M_AT["wo", b, t]))
                    else:
                        dve.wait_ge((x1_done, x2_done)[what - 2], n + 1)
                    link(dve.bn_stats(st[:, at % 2, :], x_tok[:, n, :]))
                    dve.bn_aggr(mv[:, i, :], st[:, at % 2, :]).then_inc(stats_done, 1)
                elif kind == "w1":
                    dve.wait_ge(w1_hi_done, t + 1)
                    dve.tensor_tensor(w1_lo[:, t, :], w1_raw[:, t, :], f32(w1_hi[:, t, :]),
                                      ALU.subtract).then_inc(w1_split, 1)
                elif kind == "mask_attn":
                    m = M_AT["attn", 0, t]
                    if t == 0:
                        dve.wait_ge(ld["sparse"], 16)
                    dve.wait_ge(m_done, m + 1)
                    dve.tensor_tensor(attn_f[:, t, :], m_bank[m % M_BANKS][:, :], sparse[:, t, :],
                                      ALU.mult).then_inc(m_dve, 1)
                elif kind == "split_attn":
                    dve.wait_ge(attn_hi_done, t + 1)
                    dve.tensor_tensor(attn_lo[:, t, :], attn_f[:, t, :], f32(attn_hi[:, t, :]),
                                      ALU.subtract).then_inc(attn_split, 1)
                elif kind == "onehot":
                    dve.wait_ge(consts, 8)
                    dve.wait_ge(ld["small"], 96)
                    dve.tensor_scalar(onehot[:, :], assign, cluster[:, 0:1], None, ALU.is_equal)\
                       .then_inc(onehot_done, 1)
                elif kind == "x1":
                    dve.wait_ge(*m_freed(M_AT["y1", b, t]))
                    dve.tensor_tensor(x_tok[:, n, :], x_tok[:, n, :], gelu[:, n % 2, :], ALU.add).then_inc(x1_done, 1)
                elif kind in ("x2", "out"):
                    late = kind == "out"
                    if masked_by_vector(kind, b, t):
                        dve.wait_ge(*m_freed(M_AT["mask4" if late else "mask2", 0, 0]))
                        dve.wait_ge(*m_freed(M_AT["dn4" if late else "dn2", b, t]))
                        link(dve.tensor_tensor(y_tok[:, n, :], y_tok[:, n, :], rows[:, :], ALU.mult))
                    else:
                        dve.wait_ge(y_masked, MASK_AT[kind, b, t] + 1)
                    dve.scalar_tensor_tensor(out=x_tok[:, n, :], in0=y_tok[:, n, :], scalar=qsel[:, int(late), n:n + 1],
                                             in1=x_tok[:, n, :], op0=ALU.mult, op1=ALU.add)\
                       .then_inc(out_done if late else x2_done, 1)
                elif kind in ("lo_q", "lo_k"):
                    c = ("lo_q", "lo_k").index(kind)
                    m = M_AT["qk"[c], b, 0]
                    hi, lo = ((q_hi, q_lo), (k_hi, k_lo))[c]
                    dve.wait_ge(m_hi, 3 * b + c + 1)
                    dve.scalar_tensor_tensor(out=lo, in0=m_bank[m % M_BANKS][:, :], scalar=bqkv[:, c:c + 1],
                                             in1=f32(hi), op0=ALU.add, op1=ALU.subtract).then_inc(m_dve, 1)
                elif kind == "lo_o":
                    m = M_AT["pv", b, 0]
                    dve.wait_ge(m_hi, 3 * b + 3)
                    dve.tensor_tensor(o_lo, m_bank[m % M_BANKS][:, :], f32(o_hi), ALU.subtract).then_inc(m_dve, 1)
                elif kind == "exp":
                    m = M_AT["sc", b, t]
                    dve.wait_ge(m_done, m + 1)
                    link(dve.tensor_reduce(out=mx[:, n:n + 1], in_=m_bank[m % M_BANKS][:, :], op=ALU.max, axis=AX.X))
                    dve.tensor_scalar(nmx[:, n:n + 1], mx[:, n:n + 1], -SCALE, None, ALU.mult).then_inc(max_done, 1)
                elif kind == "x3":
                    m = M_AT["wo", b, t]
                    dve.wait_ge(*m_freed(M_AT["sc", b, t]))
                    link(dve.reciprocal(rden[:, n:n + 1], den[:, n:n + 1]))
                    dve.wait_ge(m_done, m + 1)
                    dve.wait_ge(bo_added, BIAS_AT[b, t] + 1)
                    dve.scalar_tensor_tensor(out=x_tok[:, n, :], in0=m_bank[m % M_BANKS][:, :],
                                             scalar=rden[:, n:n + 1], in1=x_tok[:, n, :],
                                             op0=ALU.mult, op1=ALU.add).then_inc(m_dve, 1)
                elif kind in ("logit2", "logit4"):
                    tc = T_AT["tc" + kind[-1], b, 0]
                    at = SOFT.index((kind[-1], b))
                    bank = t_bank[tc % T_BANKS][:, :].rearrange("p (t h c) -> p t c h", t=TPB, h=2)
                    dve.wait_ge(t_done, tc + 1)
                    if at:
                        dve.wait_ge(c_exp, at)
                    dve.tensor_reduce(out=cl[:, :, :], in_=bank, op=ALU.add, axis=AX.X).then_inc(t_free, 1)
                    dve.wait_ge(t_free, tc + 1)
                    link(dve.tensor_reduce(out=cmx[:, :], in_=cl[:, :, :], op=ALU.max, axis=AX.X))
                    dve.tensor_tensor(cl[:, :, :], cl[:, :, :], cmx[:, :].unsqueeze(2).broadcast_to([P, TPB, NC]),
                                      ALU.subtract).then_inc(c_shift, 1)
                elif kind in ("prob2", "prob4"):
                    at = SOFT.index((kind[-1], b))
                    late = kind == "prob4"
                    dve.wait_ge(c_exp, at + 1)
                    link(dve.tensor_reduce(out=csum[:, :], in_=ce[:, :, :], op=ALU.add, axis=AX.X))
                    link(dve.reciprocal(crec[:, :], csum[:, :]))
                    link(dve.tensor_tensor(cl[:, :, :], ce[:, :, :], crec[:, :].unsqueeze(2).broadcast_to([P, TPB, NC]),
                                           ALU.mult))
                    dve.tensor_scalar(qsel[:, int(late), b * TPB:(b + 1) * TPB], crec[:, :], THRESHOLD, None, ALU.is_gt)
                    if late and b == 0:
                        link(dve.tensor_copy(best[:, :, :], cl[:, :, :]))
                    else:
                        link(dve.tensor_tensor(best[:, :, :], best[:, :, :], cl[:, :, :], ALU.max))
                elif kind in ("best2", "best4"):
                    tm = T_AT[kind, 0, 0]
                    dve.tensor_reduce(out=best1[:, :], in_=best[:, :, :].rearrange("p t c -> p c t"), op=ALU.max,
                                      axis=AX.X).then_inc(best_done, 1)
                    dve.wait_ge(t_done, tm + 1)
                    dve.tensor_reduce(out=csel1[:, :], in_=t_bank[tm % T_BANKS][0:NC, 0:P], op=ALU.max,
                                      axis=AX.X).then_inc(t_free, 1)
                    dve.wait_ge(t_free, tm + 1)
                    dve.tensor_scalar(csel[0:NC, :], csel1[:, :].broadcast_to([NC, P]), THRESHOLD, None,
                                      ALU.is_gt).then_inc(csel_done, 1)

        @block.tensor
        def _(pe):
            pe.wait_ge(consts, 8)

            def products(bank, pairs, bias=None, first=True, last=True):
                count = 3 * len(pairs) + (bias is not None)
                n = 0
                for (a_hi, a_lo), (w_hi, w_lo) in pairs:
                    for a, w in ((a_hi, w_hi), (a_lo, w_hi), (a_hi, w_lo)):
                        ins = pe.matmul(bank[:, :], a, w, start=(first and n == 0), stop=(last and n == count - 1))
                        n += 1
                if bias is not None:
                    pe.wait_ge(bias_split, 2)
                    ins = pe.matmul(bank[:, :], ones[:, :], bias[:, :], start=False, stop=True)
                return ins

            def t_free_for(j):
                if j >= T_BANKS:
                    pe.wait_ge(t_free, j - T_BANKS + 1)
                return t_bank[j % T_BANKS]

            def m_free_for(m):
                if m >= M_BANKS:
                    pe.wait_ge(*m_freed(m - M_BANKS))
                return m_bank[m % M_BANKS]

            def split_ready(what, b, t):
                pe.wait_ge(t_free, T_AT[what, b, t] + 1)

            for kind, what, b, t in STEPS:
                n = b * TPB + t
                if kind == "T":
                    j = T_AT[what, b, t]
                    bank = t_free_for(j)
                    if what in ("x1", "x2", "x3", "x4"):
                        stage = int(what[1])
                        src = (xn_odd, xn_even)[(stage - 1) % 2][:, t, :]
                        pe.wait_ge(norm_done, NORM_AT[stage, b, t] + 1)
                        blocks = [src[:, c * P:(c + 1) * P] for c in range(KC)]
                    elif what in ("w2", "ffn"):
                        raw = w2_raw if what == "w2" else ffn_raw
                        if t == 0:
                            pe.wait_ge(ld[what], 16)
                        blocks = [raw[:, c, t * P:(t + 1) * P] for c in range(KC)]
                    elif what == "cen":
                        pe.wait_ge(ld["cen"], 16)
                        blocks = [cen_raw[:, c * P:(c + 1) * P] for c in range(KC)]
                    elif what == "v":
                        pe.wait_ge(*m_freed(M_AT["v", b, 0]))
                        blocks = [vt[:, c * P:(c + 1) * P] for c in range(KC)]
                    elif what == "p":
                        pe.wait_ge(*m_freed(M_AT["sc", b, t]))
                        blocks = [p_tok[:, t, c * P:(c + 1) * P] for c in range(KC)]
                    else:
                        pe.wait_ge(*m_freed(M_AT["cl" + what[-1], b, 0]))
                        blocks = [lg[:, c * P:(c + 1) * P] for c in range(TPB)]
                    for c, blk in enumerate(blocks):
                        r = blk.shape[0]
                        ins = pe.transpose(bank[:, c * r:(c + 1) * r], blk, ident[0:r, 0:r])
                    ins.then_inc(t_done, 1)
                elif kind == "M":
                    m = M_AT[what, b, t]
                    bank = m_free_for(m)
                    cols = slice(t * P, (t + 1) * P)
                    if what == "attn":
                        for c in range(KC):
                            if t == 0:
                                pe.wait_ge(w1_split, c + 1)
                                split_ready("w2", 0, c)
                            ins = products(bank, [((w1_hi[:, c, cols], w1_lo[:, c, cols]),
                                                   (w2t_hi[:, c, :], w2t_lo[:, c, :]))], first=c == 0, last=c == KC - 1)
                    elif what == "y1":
                        if b == 0 and t == 0:
                            pe.wait_ge(attn_split, KC)
                        split_ready("x1", b, t)
                        ins = products(bank, [((odd_hi[:, c, cols], odd_lo[:, c, cols]),
                                               (attn_hi[:, c, :], attn_lo[:, c, :])) for c in range(KC)], bias1)
                    elif what in ("cl2", "cl4"):
                        if what == "cl2" and b == 0:
                            split_ready("cen", 0, 0)
                        split_ready("x" + what[-1], b, TPB - 1)
                        for c in range(KC):
                            for h, a in enumerate(clustered_in(b)):
                                ins = pe.matmul(bank[:, :], cen_hl[:, c, :], a[:, c, :],
                                                start=(c + h == 0), stop=(c == KC - 1 and h == 1))
                    elif what in ("dn2", "dn4"):
                        if what == "dn2" and n == 0:
                            split_ready("ffn", 0, KC - 1)
                        hi, lo = clustered_in(b)
                        ins = products(bank, [((hi[:, c, cols], lo[:, c, cols]),
                                               (ffn_hi[:, c, :], ffn_lo[:, c, :])) for c in range(KC)], bias2)
                    elif what in ("q", "k", "v"):
                        w = slice("qkv".index(what) * DH, ("qkv".index(what) + 1) * DH)
                        if b == 0 and what == "q":
                            pe.wait_ge(late_split, 2 * KC + 2)
                        if what == "q":
                            split_ready("x3", b, TPB - 1)
                        ins = products(bank, [((wqkv_hi[:, c, w], wqkv_lo[:, c, w]),
                                               (odd_hi[:, c, :], odd_lo[:, c, :])) for c in range(KC)])
                    elif what == "sc":
                        if t == 0:
                            pe.wait_ge(*m_freed(M_AT["k", b, 0]))
                        ins = products(bank, [((q_hi[:, cols], q_lo[:, cols]), (k_hi, k_lo))])
                    elif what == "pv":
                        split_ready("v", b, 0)
                        split_ready("p", b, TPB - 1)
                        ins = products(bank, [((v_hi[:, c * P:(c + 1) * P], v_lo[:, c * P:(c + 1) * P]),
                                               (pt_hi[:, c, :], pt_lo[:, c, :])) for c in range(KC)])
                    elif what == "wo":
                        if t == 0:
                            pe.wait_ge(*m_freed(M_AT["pv", b, 0]))
                        ins = products(bank, [((o_hi[:, cols], o_lo[:, cols]), (wo_hi[:, :], wo_lo[:, :]))])
                    ins.then_inc(m_done, 1)
                elif kind in ("best2", "best4"):
                    j = T_AT[kind, 0, 0]
                    bank = t_free_for(j)
                    pe.wait_ge(best_done, 1 + (kind == "best4"))
                    pe.transpose(bank[0:NC, 0:P], best1[:, :], ident[:, :]).then_inc(t_done, 1)
                elif kind in ("mask2", "mask4"):
                    m = M_AT[kind, 0, 0]
                    bank = m_free_for(m)
                    pe.wait_ge(csel_done, 1 + (kind == "mask4"))
                    pe.wait_ge(onehot_done, 1)
                    pe.matmul(bank[:, :], csel[:, :], onehot[:, :], start=True, stop=True).then_inc(m_done, 1)


_INS = ["L0_attn_a_x", "L0_attn_a_w1", "L0_attn_a_w2", "L0_attn_a_b2", "L0_attn_a_sparse_mask", "L0_attn_b_Wqkv",
        "L0_attn_b_bqkv", "L0_attn_b_Wo", "L0_attn_b_bo", "L0_ffn_weight", "L0_ffn_bias", "L0_ffn_centroids",
        "L0_ffn_assignments"]


def kernel(**inputs):
    import numpy as np
    import concourse.bacc as bacc
    from concourse.bass_utils import run_bass_kernel_spmd

    nc = bacc.Bacc("TRN2", target_bir_lowering=False, num_devices=1)
    arrays, args = {}, []
    for name in _INS:
        a = np.ascontiguousarray(inputs[name])
        arrays[f"in_{name}"] = a
        args.append(nc.dram_tensor(f"in_{name}", a.shape, mybir.dt.from_np(a.dtype), kind="ExternalInput").ap())
    out = nc.dram_tensor("out", (NB, S, D), F32, kind="ExternalOutput").ap()
    program(nc, *args, out)
    r = run_bass_kernel_spmd(nc, [arrays], core_ids=[0])
    return r.results[0]["out"]
```

```python
from contextlib import ExitStack

import concourse.bass as bass
from concourse import mybir

F32 = mybir.dt.float32
F32R = mybir.dt.float32r
I32 = mybir.dt.int32
ALU = mybir.AluOpType
ACT = mybir.ActivationFunctionType
AX = mybir.AxisListType

P = 128
NB, S, D = 4, 512, 512
TPB = S // P
NT = NB * TPB
KC = D // P
DH = D // 4
NC = 64
EPS = 1e-5
THRESHOLD = 0.01
INV_TEMPERATURE = 10.0
SCALE = float(DH) ** -0.5
T_BANKS = 4
M_BANKS = 4

FREED_BY_VECTOR = ("attn", "q", "k", "pv", "wo")


def schedule():
    o = []
    dense = []

    def step(*s):
        kind, what, b, t = s
        lag = 6 if dense and dense[0][0] == "dn2" and len(dense) > 2 else 1
        if kind == "M" and len(dense) > lag:
            o.append(("bias_f",) + dense.pop(0))
        while kind in ("blend", "masked") and any(d[1:] == (b, t) for d in dense):
            o.append(("bias_f",) + dense.pop(0))
        o.append(s)
        if kind == "M" and what in ("dn2", "dn4"):
            dense.append(s[1:])

    def transposed(what, b, t):
        step("T", what, b, t)
        step("lo", what, b, t)

    def residual(what, stage, b, t):
        step(what, "", b, t)
        step("stats", stage, b, t)

    for c in range(KC):
        step("T", "w2", 0, c)
        step("w1", "", 0, c)
        step("lo", "w2", 0, c)
    for c in range(KC - 1):
        step("M", "attn", 0, c)
    step("stats", 1, 0, 0)
    step("stats", 1, 0, 1)
    step("biases", "", 0, 0)
    step("stats", 1, 0, 2)
    step("norm", 1, 0, 0)
    step("stats", 1, 0, 3)
    step("norm", 1, 0, 1)
    step("T", "x1", 0, 0)
    step("T", "x1", 0, 1)
    step("norm", 1, 0, 2)
    step("lo", "x1", 0, 0)
    step("lo", "x1", 0, 1)
    step("norm", 1, 0, 3)
    step("M", "attn", 0, KC - 1)
    step("mask_attn", "", 0, 0)
    for t in range(1, TPB):
        step("mask_attn", "", 0, t)
        step("split_attn", "", 0, t - 1)
    step("split_attn", "", 0, TPB - 1)
    step("T", "x1", 0, 2)
    step("T", "x1", 0, 3)
    for t in range(2, TPB):
        step("lo", "x1", 0, t)
    step("onehot", "", 0, 0)
    for t in range(TPB):
        step("T", "ffn", 0, t)
        if t:
            step("norm", 1, 1, t - 1)
        if t >= 2:
            step("T", "x1", 1, t - 2)
        step("M", "y1", 0, t)
        if t:
            residual("x1", 2, 0, t - 1)
        step("lo", "ffn", 0, t)
        if t >= 2:
            step("lo", "x1", 1, t - 2)
        step("stats", 1, 1, t)
        if t >= 2:
            step("norm", 2, 0, t - 2)
    transposed("cen", 0, 0)

    for b in range(1, NB):
        for t in range(TPB):
            jobs = []
            if b == 1 and t < 2:
                jobs.append(("x1", 1, t + 2))
            if b == 1 or t + 1 < TPB:
                jobs.append(("x2", b - 1, t + (b > 1)))
            for job in jobs:
                step("T", *job)
            if b == 1 and t == 0:
                step("norm", 1, 1, TPB - 1)
            step("M", "y1", b, t)
            if t:
                residual("x1", 2, b, t - 1)
            elif b == 1:
                residual("x1", 2, 0, TPB - 1)
            for job in jobs:
                step("lo", *job)
            if b == 1 and t == 0:
                step("norm", 2, 0, TPB - 2)
            elif b == 1 and t == 1:
                step("norm", 2, 0, TPB - 1)
            elif t >= 2:
                step("norm", 2, b, t - 2)
            if b + 1 < NB:
                step("stats", 1, b + 1, t)
                if t:
                    step("norm", 1, b + 1, t - 1)
        step("M", "cl2", b - 1, 0)
        residual("x1", 2, b, TPB - 1)
        step("norm", 2, b, TPB - 2)
        if b + 1 < NB:
            step("norm", 1, b + 1, TPB - 1)
            for t in range(TPB):
                step("T", "x1", b + 1, t)
                if t == TPB - 1:
                    step("T", "x2", b, 0)
                step("M", "dn2", b - 1, t)
                if t == 0:
                    step("norm", 2, b, TPB - 1)
                step("lo", "x1", b + 1, t)
                if t == TPB - 1:
                    step("lo", "x2", b, 0)
                if t == 0:
                    step("T", "tc2", b - 1, 0)
                    step("logit2", "", b - 1, 0)
                if t == 2:
                    step("prob2", "", b - 1, 0)
    b = NB - 1
    step("T", "x2", b, 0)
    step("T", "x2", b, 1)
    step("norm", 2, b, TPB - 1)
    step("lo", "x2", b, 0)
    step("M", "dn2", b - 1, 0)
    step("lo", "x2", b, 1)
    step("T", "tc2", b - 1, 0)
    step("T", "x2", b, 2)
    step("T", "x2", b, 3)
    step("logit2", "", b - 1, 0)
    step("lo", "x2", b, 2)
    step("lo", "x2", b, 3)
    step("M", "dn2", b - 1, 1)
    for t in range(TPB):
        step("blend", 2, 0, t)
    step("prob2", "", b - 1, 0)
    last_batch_clusters(step, 2)
    residual("x2", 3, 0, 0)
    residual("x2", 3, 0, 1)
    step("norm", 3, 0, 0)
    residual("x2", 3, 0, 2)
    step("norm", 3, 0, 1)
    step("M", "dn2", b, TPB - 1)
    step("T", "x3", 0, 0)
    residual("x2", 3, 0, 3)
    step("norm", 3, 0, 2)
    step("T", "x3", 0, 1)
    step("lo", "x3", 0, 0)
    step("norm", 3, 0, 3)
    step("lo", "x3", 0, 1)
    step("T", "x3", 0, 2)
    step("rows", "", 0, 0)
    step("early", "q", 0, 0)
    step("early", "k", 0, 0)
    step("T", "x3", 0, 3)
    step("lo", "x3", 0, 2)
    step("early", "v", 0, 0)
    step("lo", "x3", 0, 3)
    blends = [("blend", 4, *divmod(n, TPB)) for n in range(NT - TPB)]
    for b in range(NB):
        step("M", "q", b, 0)
        if b:
            residual("x3", 4, b - 1, TPB - 1)
            step("norm", 4, b - 1, TPB - 2)
            transposed("x4", b - 1, 0)
        step("M", "k", b, 0)
        step("lo_q", "", b, 0)
        if b:
            step("norm", 4, b - 1, TPB - 1)
            transposed("x4", b - 1, 1)
        step("M", "v", b, 0)
        step("lo_k", "", b, 0)
        if b + 1 < NB:
            for t in range(TPB):
                step("bias_o", "", b, t)
                step("masked", "x2", b + 1, t)
            while b == 0 and dense:
                o.append(("bias_f",) + dense.pop(0))
        else:
            for t in range(TPB):
                step("bias_o", "", b, t)
        if b:
            transposed("x4", b - 1, 2)
            transposed("x4", b - 1, 3)
        for t in range(TPB):
            step("M", "sc", b, t)
            if t == 0:
                step("T", "v", b, 0)
            step("exp", "", b, t)
            if t == 0:
                step("lo", "v", b, 0)
        fill = [("dn4", b - 1, t) for t in range(TPB - 1)] if b else [("dn2", NB - 2, 2), ("dn2", NB - 2, 3)]
        if b == NB - 1:
            fill = fill[:2]
        if b:
            step("M", "cl4", b - 1, 0)
        if b + 1 < NB:
            residual("x2", 3, b + 1, 0)
        if b >= 2:
            for blend in blends[(b - 2) * TPB:(b - 2) * TPB + 2]:
                step(*blend)
        step("T", "p", b, 0)
        if len(fill) > 1:
            step("M", *fill.pop(0))
        step("lo", "p", b, 0)
        if b >= 2:
            for blend in blends[(b - 2) * TPB + 2:(b - 1) * TPB]:
                step(*blend)
        if b and b < NB - 1:
            step("T", "tc4", b - 1, 0)
            step("logit4", "", b - 1, 0)
        if b + 1 < NB:
            residual("x2", 3, b + 1, 1)
        step("T", "p", b, 1)
        if b + 1 < NB:
            step("norm", 3, b + 1, 0)
        if len(fill) > 1:
            step("M", *fill.pop(0))
        step("lo", "p", b, 1)
        step("T", "p", b, 2)
        step("T", "p", b, 3)
        step("lo", "p", b, 2)
        step("lo", "p", b, 3)
        if b + 1 < NB:
            step("norm", 3, b + 1, 1)
            residual("x2", 3, b + 1, 2)
            residual("x2", 3, b + 1, TPB - 1)
        else:
            step("T", "tc4", b - 1, 0)
            step("logit4", "", b - 1, 0)
            step("prob4", "", b - 1, 0)
        step("M" if b < NB - 1 else "early", *fill.pop(0))
        if b + 1 < NB:
            step("T", "x3", b + 1, 0)
            step("norm", 3, b + 1, 2)
            step("lo", "x3", b + 1, 0)
        step("M", "pv", b, 0)
        if b + 1 < NB:
            step("T", "x3", b + 1, 1)
            step("T", "x3", b + 1, 2)
            step("norm", 3, b + 1, TPB - 1)
            if b:
                step("M", "dn4", b - 1, TPB - 1)
        else:
            step("M", "dn4", b - 1, 1)
        step("lo_o", "", b, 0)
        if b + 1 < NB:
            step("lo", "x3", b + 1, 1)
            step("lo", "x3", b + 1, 2)
        if b and b < NB - 1:
            step("T", "x3", b + 1, TPB - 1)
            step("prob4", "", b - 1, 0)
        for t in range(TPB):
            step("M", "wo", b, t)
            if b == 0 and t == 0:
                step("T", "x3", b + 1, TPB - 1)
        if b + 1 < NB:
            step("lo", "x3", b + 1, TPB - 1)
        for t in range(TPB - 1):
            residual("x3", 4, b, t)
            if t:
                step("norm", 4, b, t - 1)
    b = NB - 1
    step("M", "dn4", b - 1, 2)
    step("T", "x4", b, 0)
    residual("x3", 4, b, TPB - 1)
    step("norm", 4, b, TPB - 2)
    step("T", "x4", b, 1)
    step("lo", "x4", b, 0)
    step("norm", 4, b, TPB - 1)
    step("lo", "x4", b, 1)
    step("M", "dn4", b - 1, 3)
    step("T", "x4", b, 2)
    step("T", "x4", b, 3)
    for blend in blends[2 * TPB:2 * TPB + 1]:
        step(*blend)
    step("lo", "x4", b, 2)
    step("lo", "x4", b, 3)
    for blend in blends[2 * TPB + 1:2 * TPB + 3]:
        step(*blend)
    last_batch_clusters(step, 4)
    step("M", "dn4", b, TPB - 1)
    step("blend", 4, b, 0)
    for n in range(NT):
        if n in (NT - 6, NT - 4, NT - 2):
            step("blend", 4, b, (n - NT + 8) // 2)
        step("out", "", *divmod(n, TPB))
    return o


def last_batch_clusters(step, stage):
    b, dense = NB - 1, f"dn{stage}"
    if stage == 4:
        step("early", "cl4", b, 0)
    step("M", f"cl{stage}", b, 0)
    step("T", f"tc{stage}", b, 0)
    step(f"logit{stage}", "", b, 0)
    if stage == 4:
        step("blend", 4, b - 1, TPB - 1)
    step("M", dense, b, 0)
    step("M", dense, b, 1)
    step(f"prob{stage}", "", b, 0)
    step(f"best{stage}", "", 0, 0)
    step(f"mask{stage}", "", 0, 0)
    step("M", dense, b, 2)


def program(nc, x_d, w1_d, w2_d, b2_d, sparse_d, wqkv_d, bqkv_d, wo_d, bo_d, ffn_d, fb_d, cen_d,
            assign_d, out_d):
    STEPS = schedule()
    T_AT = {}
    M_AT = {}
    for s in STEPS:
        if s[0] == "T":
            T_AT[s[1:]] = len(T_AT)
        if s[0] in ("best2", "best4"):
            T_AT[s[0], 0, 0] = len(T_AT)
        if s[0] in ("mask2", "mask4"):
            M_AT[s[0], 0, 0] = len(M_AT)
        if s[0] == "M":
            M_AT[s[1:]] = len(M_AT)
    M_JOBS = list(M_AT)
    STAT_AT = {s[1:]: n for n, s in enumerate([s for s in STEPS if s[0] == "stats"])}
    MASK_AT = {s[1:]: n for n, s in enumerate([s for s in STEPS if s[0] == "masked"])}
    BIAS_F_AT = {s[1:]: n for n, s in enumerate([s for s in STEPS if s[0] == "bias_f"])}
    BLEND_AT = {s[1:]: n for n, s in enumerate([s for s in STEPS if s[0] == "blend"])}
    BIAS_AT = {s[2:]: n for n, s in enumerate([s for s in STEPS if s[0] == "bias_o"])}
    NORM_AT = {s[1:]: n for n, s in enumerate([s for s in STEPS if s[0] == "norm"])}
    HI_JOBS = [j for j in T_AT if j[0] not in ("tc2", "tc4", "best2", "best4")]
    HI_AT = {j: n for n, j in enumerate(HI_JOBS)}
    SOFT = [(s[0][-1], s[2]) for s in STEPS if s[0] in ("logit2", "logit4")]

    assert list(T_AT.values()) == [T_AT[j] for j in [
        (s[1:] if s[0] == "lo" else ("tc" + s[0][-1], s[2], 0) if s[0] in ("logit2", "logit4") else (s[0], 0, 0))
        for s in STEPS if s[0] in ("lo", "logit2", "logit4", "best2", "best4")]]

    ctx = ExitStack()
    with ctx:
        def sb(name, shape, dt=F32):
            return ctx.enter_context(nc.sbuf_tensor(name, shape, dt))

        def sem(name):
            return ctx.enter_context(nc.semaphore(name))

        x_tok = sb("x_tok", [P, NT, D])
        y_tok = sb("y_tok", [P, NT, D])
        odd_hi = sb("odd_hi", [P, KC, S], F32R)
        odd_lo = sb("odd_lo", [P, KC, S], F32R)
        even_hi = sb("even_hi", [P, KC, S], F32R)
        even_lo = sb("even_lo", [P, KC, S], F32R)
        xn_odd = sb("xn_odd", [P, TPB, D])
        xn_even = sb("xn_even", [P, TPB, D])
        w2_raw = sb("w2_raw", [P, KC, D])
        w1_raw = y_tok[:, KC:2 * KC, :]
        ffn_raw = w2_raw
        w1_hi, w1_lo = even_hi, even_lo
        w2t_hi = sb("w2t_hi", [P, KC, D], F32R)
        w2t_lo = sb("w2t_lo", [P, KC, D], F32R)
        pt_hi, pt_lo = w2t_hi, w2t_lo
        sparse = y_tok[:, NT - 2 * KC:NT - KC, :]
        attn_f = y_tok[:, NT - KC:NT, :]
        attn_hi = sb("attn_hi", [P, KC, D], F32R)
        attn_lo = sb("attn_lo", [P, KC, D], F32R)
        ffn_hi = sb("ffn_hi", [P, KC, D], F32R)
        ffn_lo = sb("ffn_lo", [P, KC, D], F32R)
        cen_hl = sb("cen_hl", [P, KC, 2 * NC], F32R)
        wqkv_raw = y_tok[:, 2 * KC:3 * KC, 0:3 * DH]
        wo_raw = y_tok[:, NT - 3, :]
        wqkv_hi = sb("wqkv_hi", [P, KC, 3 * DH], F32R)
        wqkv_lo = sb("wqkv_lo", [P, KC, 3 * DH], F32R)
        wo_hi = sb("wo_hi", [P, D], F32R)
        wo_lo = sb("wo_lo", [P, D], F32R)
        p_tok = w2_raw
        gelu = y_tok[:, NT - 2:NT, :]
        q_hi = attn_hi[:, 0, :]
        q_lo = attn_hi[:, 1, :]
        k_hi = attn_hi[:, 2, :]
        k_lo = attn_hi[:, 3, :]
        v_hi = attn_lo[:, 0, :]
        v_lo = attn_lo[:, 1, :]
        o_hi = attn_lo[:, 2, :]
        o_lo = attn_lo[:, 3, :]
        vt = sb("vt", [P, S])
        lg = sb("lg", [P, S])
        cen_raw = lg[0:NC, :]
        cl = sb("cl", [P, TPB, NC])
        ce = sb("ce", [P, TPB, NC])
        best = sb("best", [P, TPB, NC])
        best1 = sb("best1", [P, NC])
        onehot = sb("onehot", [P, D], F32R)
        assign = y_tok[:, 2, :].bitcast(I32)
        cluster = sb("cluster", [P, 1])
        csel = sb("csel", [P, P], F32R)
        csel1 = sb("csel1", [NC, 1])
        rows = sb("rows", [P, D])
        ident = sb("ident", [P, P])
        ones = sb("ones", [P, P], F32R)
        bias1 = sb("bias1", [P, D], F32R)
        bias_f = sb("bias_f", [P, D])
        bias_raw = y_tok[0:33, 0, :]
        bqkv = sb("bqkv", [P, 3])
        bo = sb("bo", [P, D])
        half = sb("half", [P, 1])
        st = sb("st", [P, 2, 6])
        mv = sb("mv", [P, 4 * NT, 2])
        ve = sb("ve", [P, 4 * NT])
        rstd = sb("rstd", [P, 4 * NT])
        nbias = sb("nbias", [P, 4 * NT])
        mx = sb("mx", [P, NT])
        nmx = sb("nmx", [P, NT])
        den = sb("den", [P, NT])
        rden = sb("rden", [P, NT])
        cmx = sb("cmx", [P, TPB])
        csum = sb("csum", [P, TPB])
        crec = sb("crec", [P, TPB])
        qsel = sb("qsel", [P, 2, NT])

        t_bank = [ctx.enter_context(nc.psum_tensor(f"t_bank{i}", [P, 512], F32)) for i in range(T_BANKS)]
        m_bank = [ctx.enter_context(nc.psum_tensor(f"m_bank{i}", [P, 512], F32)) for i in range(M_BANKS)]

        ld = {k: sem("ld_" + k) for k in ("sparse", "x0", "x1", "x2", "x3", "ffn", "cen",
                                          "wqkv", "wo", "small", "rows", "bias", "bias_f")}
        ld_w2 = [sem(f"ld_w2_{c}") for c in range(KC)]
        ld_w1 = [sem(f"ld_w1_{c}") for c in range(KC)]
        consts = sem("consts")
        t_done = sem("t_done")
        t_hi = sem("t_hi")
        t_free = sem("t_free")
        m_done = sem("m_done")
        m_act = sem("m_act")
        m_dve = sem("m_dve")
        m_hi = sem("m_hi")
        stats_done = sem("stats_done")
        rstd_done = sem("rstd_done")
        norm_done = sem("norm_done")
        w1_hi_done = sem("w1_hi_done")
        w1_split = sem("w1_split")
        attn_hi_done = sem("attn_hi_done")
        attn_split = sem("attn_split")
        bias_hi = sem("bias_hi")
        bias_split = sem("bias_split")
        late_split = sem("late_split")
        x1_done = sem("x1_done")
        x2_done = sem("x2_done")
        out_done = sem("out_done")
        bo_added = sem("bo_added")
        biased = sem("biased")
        y_masked = sem("y_masked")
        max_done = sem("max_done")
        c_shift = sem("c_shift")
        c_exp = sem("c_exp")
        csel_done = sem("csel_done")
        rows_done = sem("rows_done")
        blended = sem("blended")
        queries_done = sem("queries_done")
        best_done = sem("best_done")
        onehot_done = sem("onehot_done")
        chain = sem("chain")
        pchain = sem("pchain")
        stored = sem("stored")

        def m_freed(m):
            if M_JOBS[m][0] == "mask2":
                return rows_done, 1
            dve = M_JOBS[m][0] in FREED_BY_VECTOR
            n = sum((j[0] in FREED_BY_VECTOR) == dve and j[0] not in ("mask2", "mask4") for j in M_JOBS[:m + 1])
            return (m_dve if dve else m_act), n

        def feat(tensor, t):
            return tensor[:, :, t * P:(t + 1) * P]

        def clustered_in(b):
            return (odd_hi, odd_lo) if b == NB - 1 else (even_hi, even_lo)

        def f32(ap):
            return ap.bitcast(F32)

        def split_of(what, b, t):
            if what in ("x1", "x3"):
                return feat(odd_hi, t), feat(odd_lo, t)
            if what in ("x2", "x4"):
                hi, lo = clustered_in(b)
                return feat(hi, t), feat(lo, t)
            if what == "w2":
                return w2t_hi[:, t, :], w2t_lo[:, t, :]
            if what == "ffn":
                return ffn_hi[:, t, :], ffn_lo[:, t, :]
            if what == "cen":
                return cen_hl[:, :, 0:NC], cen_hl[:, :, NC:2 * NC]
            if what == "v":
                return v_hi, v_lo
            return feat(pt_hi, t), feat(pt_lo, t)

        def bank_view(what, bank):
            if what == "cen":
                return bank[:, 0:KC * NC].rearrange("p (k c) -> p k c", k=KC)
            if what in ("w2", "ffn", "v"):
                return bank[:, :]
            return bank[:, :].rearrange("p (k c) -> p k c", k=KC)

        block = ctx.enter_context(nc.Block())

        @block.sync
        def _(sp):
            rows_of = lambda d: d.rearrange("(c p) n -> p c n", p=P)

            def load_x(b):
                sp.dma_start(x_tok[:, b * TPB:(b + 1) * TPB, :], rows_of(x_d[b])).then_inc(ld[f"x{b}"], 16)

            for c in range(KC):
                cols = slice(c * P, (c + 1) * P)
                sp.dma_start(w2_raw[:, :, cols], rows_of(w2_d[:, cols])).then_inc(ld_w2[c], 16)
                sp.dma_start(w1_raw[:, c, :], w1_d[cols, :]).then_inc(ld_w1[c], 16)
            sp.dma_start(bias_raw[0:1, :], b2_d.rearrange("(a n) -> a n", a=1)).then_inc(ld["rows"], 16)
            sp.dma_start(bias_raw[32:33, :], b2_d.rearrange("(a n) -> a n", a=1)).then_inc(ld["rows"], 16)
            sp.dma_start(bias_f[:, :], fb_d.rearrange("(a n) -> a n", a=1).broadcast_to([P, D])).then_inc(ld["bias_f"], 16)
            sp.dma_start(bqkv[:, :], bqkv_d.rearrange("(j p) -> p j", p=P),
                          allow_slow_non_contiguous=True).then_inc(ld["small"], 16)
            sp.dma_start(assign, assign_d.rearrange("(a n) -> a n", a=1).broadcast_to([P, D])).then_inc(ld["small"], 16)
            sp.dma_start(bo[:, :], bo_d.rearrange("(a n) -> a n", a=1).broadcast_to([P, D])).then_inc(ld["bias"], 16)
            load_x(0)
            sp.dma_start(sparse, rows_of(sparse_d)).then_inc(ld["sparse"], 16)
            sp.dma_start(cen_raw, cen_d).then_inc(ld["cen"], 16)
            sp.wait_ge(t_done, T_AT["w2", 0, KC - 1] + 1)
            sp.dma_start(ffn_raw[:, :, :], rows_of(ffn_d)).then_inc(ld["ffn"], 16)
            load_x(1)
            sp.wait_ge(attn_split, KC)
            sp.dma_start(wo_raw, wo_d).then_inc(ld["wo"], 16)
            sp.dma_start(wqkv_raw, rows_of(wqkv_d)).then_inc(ld["wqkv"], 16)
            load_x(2)
            load_x(3)
            outs = [b * TPB + t for kind, _, b, t in STEPS if kind == "out"]
            for at, n in enumerate(outs):
                sp.wait_ge(out_done, at + 1)
                sp.dma_start(out_d[n // TPB, (n % TPB) * P:(n % TPB + 1) * P, :], x_tok[:, n, :]).then_inc(stored, 16)
            sp.wait_ge(stored, 16 * NT)

        @block.gpsimd
        def _(pool):
            pchained = [0]

            def link(ins):
                pchained[0] += 1
                ins.then_inc(pchain, 1)
                pool.wait_ge(pchain, pchained[0])

            pool.memset(ident[:, :], 0.0).then_inc(pchain, 1)
            pchained[0] += 1
            pool.wait_ge(pchain, 1)
            pool.affine_select(out=ident[:, :], in_=ident[:, :], compare_op=ALU.not_equal, fill=1.0,
                               base=0, pattern=[[-1, P]], channel_multiplier=1).then_inc(consts, 1)
            pool.memset(half[:, :], -0.5).then_inc(consts, 1)
            pool.memset(f32(ones[:, :]), 1.0).then_inc(consts, 1)
            pool.memset(f32(bias1[:, :]), 0.0).then_inc(consts, 1)
            pool.memset(f32(csel[:, :]), 0.0).then_inc(consts, 1)
            pool.memset(best[:, :, :], 0.0).then_inc(consts, 1)
            pool.iota(cluster[:, :], pattern=[[0, 1]], base=0, channel_multiplier=1,
                      allow_small_or_imprecise_dtypes=True).then_inc(consts, 1)

            pieces = [("hi", c) for c in range(KC + 1)] + [("lo", c) for c in range(KC + 1)]

            def split_late(part, c):
                if (part, c) == ("hi", 0):
                    pool.wait_ge(ld["wqkv"], 16)
                    pool.wait_ge(ld["wo"], 16)
                if (part, c) == ("lo", 0):
                    pool.wait_ge(late_split, KC + 1)
                raw = wo_raw if c == KC else wqkv_raw[:, c, :]
                hi = wo_hi[:, :] if c == KC else wqkv_hi[:, c, :]
                lo = wo_lo[:, :] if c == KC else wqkv_lo[:, c, :]
                if part == "hi":
                    pool.tensor_copy(hi, raw).then_inc(late_split, 1)
                else:
                    pool.tensor_tensor(lo, raw, f32(hi), ALU.subtract).then_inc(late_split, 1)

            for kind, what, b, t in STEPS:
                n = b * TPB + t
                if kind == "stats":
                    at = STAT_AT[what, b, t]
                    i = (what - 1) * NT + n
                    pool.wait_ge(stats_done, at + 1)
                    link(pool.tensor_scalar(ve[:, i:i + 1], mv[:, i, 1:2], EPS, None, ALU.add))
                    link(pool.tensor_tensor(rstd[:, i:i + 1], ve[:, i:i + 1], half[:, :], ALU.pow))
                    pool.tensor_scalar(nbias[:, i:i + 1], mv[:, i, 0:1], rstd[:, i:i + 1], -1.0, ALU.mult,
                                       ALU.mult).then_inc(rstd_done, 1)
                    if (what == 2 and b >= 1 or what == 1 and b >= 2) and pieces:
                        split_late(*pieces.pop(0))
                elif kind == "bias_f":
                    if BIAS_F_AT[what, b, t] == 0:
                        pool.wait_ge(ld["bias_f"], 16)
                    pool.wait_ge(*m_freed(M_AT[what, b, t]))
                    pool.tensor_tensor(y_tok[:, n, :], y_tok[:, n, :], bias_f[:, :], ALU.add).then_inc(biased, 1)
                elif kind == "masked" and (what, b, t) in MASK_AT:
                    pool.wait_ge(rows_done, 1)
                    pool.wait_ge(biased, BIAS_F_AT["dn2", b, t] + 1)
                    pool.tensor_tensor(y_tok[:, n, :], y_tok[:, n, :], rows[:, :], ALU.mult).then_inc(y_masked, 1)
                elif kind == "bias_o":
                    pool.wait_ge(norm_done, NORM_AT[3, b, t] + 1)
                    if n == 0:
                        pool.wait_ge(ld["bias"], 16)
                    pool.tensor_tensor(x_tok[:, n, :], x_tok[:, n, :], bo[:, :], ALU.add).then_inc(bo_added, 1)

        @block.scalar
        def _(act):
            for kind, what, b, t in STEPS:
                n = b * TPB + t
                if kind == "biases":
                    act.wait_ge(ld["rows"], 32)
                    act.wait_ge(consts, 7)
                    act.activation(bias1[32:33, :], bias_raw[32:33, :], ACT.Copy).then_inc(bias_hi, 1)
                    act.activation(bias1[0:1, :], bias_raw[0:1, :], ACT.Copy).then_inc(bias_hi, 1)
                elif kind == "w1":
                    act.wait_ge(ld_w1[t], 16)
                    act.activation(w1_hi[:, t, :], w1_raw[:, t, :], ACT.Copy).then_inc(w1_hi_done, 1)
                elif kind == "norm":
                    i = (what - 1) * NT + n
                    dst = (xn_odd, xn_even)[(what - 1) % 2]
                    act.wait_ge(rstd_done, STAT_AT[what, b, t] + 1)
                    if b:
                        act.wait_ge(t_done, T_AT[f"x{what}", b - 1, t] + 1)
                    elif what >= 3:
                        act.wait_ge(t_done, T_AT[f"x{what - 2}", NB - 1, t] + 1)
                    act.activation(dst[:, t, :], x_tok[:, n, :], ACT.Identity, bias=nbias[:, i:i + 1],
                                   scale=rstd[:, i:i + 1]).then_inc(norm_done, 1)
                elif kind == "T" and (what, b, t) in HI_AT:
                    j = T_AT[what, b, t]
                    act.wait_ge(t_done, j + 1)
                    if what == "x1" and b >= 1:
                        act.wait_ge(m_done, M_AT["y1", b - 1, t] + 1)
                    elif what == "x2" and b == NB - 1:
                        act.wait_ge(m_done, M_AT["y1", b, t] + 1)
                    elif what == "x2":
                        act.wait_ge(m_done, (M_AT["dn2", b - 1, t] if b else M_AT["attn", 0, KC - 1]) + 1)
                    elif what == "x3":
                        act.wait_ge(m_done, (M_AT["v", b - 1, 0] if b else M_AT["dn2", NB - 1, t]) + 1)
                    elif what == "x4" and b == NB - 1:
                        act.wait_ge(m_done, M_AT["v", b, 0] + 1)
                    elif what == "x4":
                        act.wait_ge(m_done, (M_AT["dn4", b - 1, t] if b else M_AT["dn2", NB - 2, t]) + 1)
                    elif what in ("p", "v") and b >= 1:
                        act.wait_ge(m_done, M_AT["pv", b - 1, 0] + 1)
                    elif what in ("p", "v"):
                        act.wait_ge(m_done, M_AT["y1", NB - 1, TPB - 1] + 1)
                    act.activation(split_of(what, b, t)[0], bank_view(what, t_bank[j % T_BANKS]), ACT.Copy).then_inc(t_hi, 1)
                elif kind == "split_attn":
                    act.wait_ge(*m_freed(M_AT["attn", 0, t]))
                    act.activation(attn_hi[:, t, :], attn_f[:, t, :], ACT.Copy).then_inc(attn_hi_done, 1)
                elif kind == "M" and what != "attn" and what != "wo":
                    m = M_AT[what, b, t]
                    bank = m_bank[m % M_BANKS]
                    if what != "sc":
                        act.wait_ge(m_done, m + 1)
                    if what == "y1":
                        if n >= 2:
                            act.wait_ge(x1_done, n - 1)
                        act.activation(gelu[:, n % 2, :], bank[:, :], ACT.Gelu).then_inc(m_act, 1)
                    elif what in ("dn2", "dn4"):
                        if what == "dn4":
                            act.wait_ge(x2_done, n + 1)
                        elif n == 2 * KC:
                            act.wait_ge(late_split, 2 * KC + 2)
                        elif n == NT - 2:
                            act.wait_ge(x1_done, NT)
                        act.activation(y_tok[:, n, :], bank[:, :], ACT.Copy).then_inc(m_act, 1)
                    elif what in ("cl2", "cl4"):
                        if what == "cl2" and b:
                            act.wait_ge(t_done, T_AT["tc2", b - 1, 0] + 1)
                        if what == "cl4":
                            act.wait_ge(t_done, (T_AT["tc4", b - 1, 0] if b else T_AT["tc2", NB - 1, 0]) + 1)
                        act.activation(lg[:, :], bank[:, :], ACT.Copy).then_inc(m_act, 1)
                    elif what in ("q", "k"):
                        if b:
                            act.wait_ge(m_done, M_AT["sc", b - 1, TPB - 1] + 1)
                        j = "qk".index(what)
                        if b == 0 and what == "q":
                            act.wait_ge(ld["small"], 32)
                        act.activation((q_hi, k_hi)[j], bank[:, :], ACT.Identity,
                                       bias=bqkv[:, j:j + 1]).then_inc(m_hi, 1)
                    elif what == "v":
                        if b:
                            act.wait_ge(t_done, T_AT["v", b - 1, 0] + 1)
                        else:
                            act.wait_ge(late_split, 2 * KC + 2)
                        act.activation(vt[:, :], bank[:, :], ACT.Identity, bias=bqkv[:, 2:3]).then_inc(m_act, 1)
                    elif what == "pv":
                        if b:
                            act.wait_ge(m_done, M_AT["wo", b - 1, TPB - 1] + 1)
                        act.activation(o_hi, bank[:, :], ACT.Copy).then_inc(m_hi, 1)
                elif kind == "exp":
                    m = M_AT["sc", b, t]
                    act.wait_ge(max_done, n + 1)
                    if b:
                        act.wait_ge(t_done, T_AT["p", b - 1, t] + 1)
                    act.activation(p_tok[:, t, :], m_bank[m % M_BANKS][:, :], ACT.Exp, bias=nmx[:, n:n + 1],
                                   scale=SCALE, accum_out=den[:, n:n + 1]).then_inc(m_act, 1)
                elif kind in ("logit2", "logit4"):
                    act.wait_ge(c_shift, SOFT.index((kind[-1], b)) + 1)
                    act.activation(ce[:, :, :], cl[:, :, :], ACT.Exp, scale=INV_TEMPERATURE).then_inc(c_exp, 1)
                elif kind == "rows":
                    m = M_AT["mask2", 0, 0]
                    act.wait_ge(x2_done, TPB)
                    act.activation(rows[:, :], m_bank[m % M_BANKS][:, :], ACT.Copy).then_inc(rows_done, 1)

        @block.vector
        def _(dve):
            chained = [0]

            def link(ins):
                chained[0] += 1
                ins.then_inc(chain, 1)
                dve.wait_ge(chain, chained[0])

            for kind, what, b, t in STEPS:
                n = b * TPB + t
                if kind == "biases":
                    dve.wait_ge(bias_hi, 2)
                    dve.tensor_tensor(bias1[32:33, :], bias_raw[32:33, :], f32(bias1[32:33, :]),
                                      ALU.subtract).then_inc(bias_split, 1)
                elif kind == "lo":
                    j = T_AT[what, b, t]
                    hi, lo = split_of(what, b, t)
                    dve.wait_ge(t_hi, HI_AT[what, b, t] + 1)
                    dve.tensor_tensor(lo, bank_view(what, t_bank[j % T_BANKS]), f32(hi), ALU.subtract).then_inc(t_free, 1)
                elif kind == "stats":
                    i = (what - 1) * NT + n
                    at = STAT_AT[what, b, t]
                    if what == 1:
                        dve.wait_ge(ld[f"x{b}"], 16)
                    elif what == 4:
                        dve.wait_ge(*m_freed(M_AT["wo", b, t]))
                    else:
                        dve.wait_ge((x1_done, x2_done)[what - 2], n + 1)
                    link(dve.bn_stats(st[:, at % 2, :], x_tok[:, n, :]))
                    dve.bn_aggr(mv[:, i, :], st[:, at % 2, :]).then_inc(stats_done, 1)
                elif kind == "w1":
                    dve.wait_ge(w1_hi_done, t + 1)
                    dve.tensor_tensor(w1_lo[:, t, :], w1_raw[:, t, :], f32(w1_hi[:, t, :]),
                                      ALU.subtract).then_inc(w1_split, 1)
                elif kind == "mask_attn":
                    m = M_AT["attn", 0, t]
                    if t == 0:
                        dve.wait_ge(ld["sparse"], 16)
                    dve.wait_ge(m_done, m + 1)
                    dve.tensor_tensor(attn_f[:, t, :], m_bank[m % M_BANKS][:, :], sparse[:, t, :],
                                      ALU.mult).then_inc(m_dve, 1)
                elif kind == "split_attn":
                    dve.wait_ge(attn_hi_done, t + 1)
                    dve.tensor_tensor(attn_lo[:, t, :], attn_f[:, t, :], f32(attn_hi[:, t, :]),
                                      ALU.subtract).then_inc(attn_split, 1)
                elif kind == "onehot":
                    dve.wait_ge(consts, 7)
                    dve.wait_ge(ld["small"], 32)
                    dve.tensor_scalar(onehot[:, :], assign, cluster[:, 0:1], None, ALU.is_equal)\
                       .then_inc(onehot_done, 1)
                elif kind == "x1":
                    dve.wait_ge(*m_freed(M_AT["y1", b, t]))
                    dve.tensor_tensor(x_tok[:, n, :], x_tok[:, n, :], gelu[:, n % 2, :], ALU.add).then_inc(x1_done, 1)
                elif kind == "blend":
                    dve.wait_ge(biased, BIAS_F_AT["dn%d" % what, b, t] + 1)
                    dve.wait_ge(queries_done, SOFT.index((str(what), b)) + 1)
                    dve.scalar_tensor_tensor(out=y_tok[:, n, :], in0=y_tok[:, n, :],
                                             scalar=qsel[:, what // 2 - 1, n:n + 1], in1=x_tok[:, n, :],
                                             op0=ALU.mult, op1=ALU.add).then_inc(blended, 1)
                elif kind == "out" or kind == "x2" and b == 0:
                    m = M_AT["mask2" if kind == "x2" else "mask4", 0, 0]
                    dve.wait_ge(m_done, m + 1)
                    dve.wait_ge(blended, BLEND_AT[2 if kind == "x2" else 4, b, t] + 1)
                    ins = dve.copy_predicated(x_tok[:, n, :], m_bank[m % M_BANKS][:, :].bitcast(I32), y_tok[:, n, :])
                    ins.then_inc(out_done if kind == "out" else x2_done, 1)
                elif kind == "x2":
                    dve.wait_ge(y_masked, MASK_AT[kind, b, t] + 1)
                    dve.scalar_tensor_tensor(out=x_tok[:, n, :], in0=y_tok[:, n, :], scalar=qsel[:, 0, n:n + 1],
                                             in1=x_tok[:, n, :], op0=ALU.mult, op1=ALU.add).then_inc(x2_done, 1)
                elif kind in ("lo_q", "lo_k"):
                    c = ("lo_q", "lo_k").index(kind)
                    m = M_AT["qk"[c], b, 0]
                    hi, lo = ((q_hi, q_lo), (k_hi, k_lo))[c]
                    dve.wait_ge(m_hi, 3 * b + c + 1)
                    dve.scalar_tensor_tensor(out=lo, in0=m_bank[m % M_BANKS][:, :], scalar=bqkv[:, c:c + 1],
                                             in1=f32(hi), op0=ALU.add, op1=ALU.subtract).then_inc(m_dve, 1)
                elif kind == "lo_o":
                    m = M_AT["pv", b, 0]
                    dve.wait_ge(*m_freed(M_AT["sc", b, TPB - 1]))
                    link(dve.reciprocal(rden[:, n:n + TPB], den[:, n:n + TPB]))
                    dve.wait_ge(m_hi, 3 * b + 3)
                    dve.tensor_tensor(o_lo, m_bank[m % M_BANKS][:, :], f32(o_hi), ALU.subtract).then_inc(m_dve, 1)
                elif kind == "exp":
                    m = M_AT["sc", b, t]
                    dve.wait_ge(m_done, m + 1)
                    link(dve.tensor_reduce(out=mx[:, n:n + 1], in_=m_bank[m % M_BANKS][:, :], op=ALU.max, axis=AX.X))
                    dve.tensor_scalar(nmx[:, n:n + 1], mx[:, n:n + 1], -SCALE, None, ALU.mult).then_inc(max_done, 1)
                elif kind == "x3":
                    m = M_AT["wo", b, t]
                    dve.wait_ge(m_done, m + 1)
                    dve.wait_ge(bo_added, BIAS_AT[b, t] + 1)
                    dve.scalar_tensor_tensor(out=x_tok[:, n, :], in0=m_bank[m % M_BANKS][:, :],
                                             scalar=rden[:, n:n + 1], in1=x_tok[:, n, :],
                                             op0=ALU.mult, op1=ALU.add).then_inc(m_dve, 1)
                elif kind in ("logit2", "logit4"):
                    tc = T_AT["tc" + kind[-1], b, 0]
                    at = SOFT.index((kind[-1], b))
                    bank = t_bank[tc % T_BANKS][:, :].rearrange("p (t h c) -> p t c h", t=TPB, h=2)
                    dve.wait_ge(t_done, tc + 1)
                    if at:
                        dve.wait_ge(c_exp, at)
                    dve.tensor_reduce(out=cl[:, :, :], in_=bank, op=ALU.add, axis=AX.X).then_inc(t_free, 1)
                    dve.wait_ge(t_free, tc + 1)
                    link(dve.tensor_reduce(out=cmx[:, :], in_=cl[:, :, :], op=ALU.max, axis=AX.X))
                    dve.tensor_tensor(cl[:, :, :], cl[:, :, :], cmx[:, :].unsqueeze(2).broadcast_to([P, TPB, NC]),
                                      ALU.subtract).then_inc(c_shift, 1)
                elif kind in ("prob2", "prob4"):
                    at = SOFT.index((kind[-1], b))
                    late = kind == "prob4"
                    dve.wait_ge(c_exp, at + 1)
                    link(dve.tensor_reduce(out=csum[:, :], in_=ce[:, :, :], op=ALU.add, axis=AX.X))
                    link(dve.reciprocal(crec[:, :], csum[:, :]))
                    link(dve.tensor_tensor(cl[:, :, :], ce[:, :, :], crec[:, :].unsqueeze(2).broadcast_to([P, TPB, NC]),
                                           ALU.mult))
                    dve.tensor_scalar(qsel[:, int(late), b * TPB:(b + 1) * TPB], crec[:, :], THRESHOLD, None,
                                      ALU.is_gt).then_inc(queries_done, 1)
                    if late and b == 0:
                        link(dve.tensor_copy(best[:, :, :], cl[:, :, :]))
                    else:
                        link(dve.tensor_tensor(best[:, :, :], best[:, :, :], cl[:, :, :], ALU.max))
                elif kind in ("best2", "best4"):
                    tm = T_AT[kind, 0, 0]
                    dve.tensor_reduce(out=best1[:, :], in_=best[:, :, :].rearrange("p t c -> p c t"), op=ALU.max,
                                      axis=AX.X).then_inc(best_done, 1)
                    dve.wait_ge(t_done, tm + 1)
                    dve.tensor_reduce(out=csel1[:, :], in_=t_bank[tm % T_BANKS][0:NC, 0:P], op=ALU.max,
                                      axis=AX.X).then_inc(t_free, 1)
                    dve.wait_ge(t_free, tm + 1)
                    dve.tensor_scalar(csel[0:NC, :], csel1[:, :].broadcast_to([NC, P]), THRESHOLD, None,
                                      ALU.is_gt).then_inc(csel_done, 1)

        @block.tensor
        def _(pe):
            pe.wait_ge(consts, 7)

            def products(bank, pairs, bias=None, first=True, last=True):
                count = 3 * len(pairs) + (bias is not None)
                n = 0
                for (a_hi, a_lo), (w_hi, w_lo) in pairs:
                    for a, w in ((a_hi, w_hi), (a_lo, w_hi), (a_hi, w_lo)):
                        ins = pe.matmul(bank, a, w, start=(first and n == 0), stop=(last and n == count - 1))
                        n += 1
                if bias is not None:
                    pe.wait_ge(bias_split, 1)
                    ins = pe.matmul(bank, ones[:, :], bias[:, :], start=False, stop=True)
                return ins

            def t_free_for(j):
                if j >= T_BANKS:
                    pe.wait_ge(t_free, j - T_BANKS + 1)
                return t_bank[j % T_BANKS]

            def m_free_for(m):
                if m >= M_BANKS:
                    pe.wait_ge(*m_freed(m - M_BANKS))
                return m_bank[m % M_BANKS][:, :]

            def split_ready(what, b, t):
                pe.wait_ge(t_free, T_AT[what, b, t] + 1)

            def columns_of(kind, what, b):
                if kind == "early":
                    return slice(0, S // 2)
                return slice(S // 2 if ("early", what, b, 0) in STEPS else 0, S)

            def chunks_of(kind, what, b, t):
                if kind == "early":
                    return range(KC // 2)
                return range(KC // 2 if ("early", what, b, t) in STEPS else 0, KC)

            for kind, what, b, t in STEPS:
                n = b * TPB + t
                if kind == "T":
                    j = T_AT[what, b, t]
                    bank = t_free_for(j)
                    if what in ("x1", "x2", "x3", "x4"):
                        stage = int(what[1])
                        src = (xn_odd, xn_even)[(stage - 1) % 2][:, t, :]
                        pe.wait_ge(norm_done, NORM_AT[stage, b, t] + 1)
                        blocks = [src[:, c * P:(c + 1) * P] for c in range(KC)]
                    elif what in ("w2", "ffn"):
                        raw = w2_raw if what == "w2" else ffn_raw
                        if what == "w2":
                            pe.wait_ge(ld_w2[t], 16)
                        elif t == 0:
                            pe.wait_ge(ld["ffn"], 16)
                        blocks = [raw[:, c, t * P:(t + 1) * P] for c in range(KC)]
                    elif what == "cen":
                        pe.wait_ge(ld["cen"], 16)
                        blocks = [cen_raw[:, c * P:(c + 1) * P] for c in range(KC)]
                    elif what == "v":
                        pe.wait_ge(*m_freed(M_AT["v", b, 0]))
                        blocks = [vt[:, c * P:(c + 1) * P] for c in range(KC)]
                    elif what == "p":
                        pe.wait_ge(*m_freed(M_AT["sc", b, t]))
                        blocks = [p_tok[:, t, c * P:(c + 1) * P] for c in range(KC)]
                    else:
                        pe.wait_ge(*m_freed(M_AT["cl" + what[-1], b, 0]))
                        blocks = [lg[:, c * P:(c + 1) * P] for c in range(TPB)]
                    for c, blk in enumerate(blocks):
                        r = blk.shape[0]
                        ins = pe.transpose(bank[:, c * r:(c + 1) * r], blk, ident[0:r, 0:r])
                    ins.then_inc(t_done, 1)
                elif kind == "M" and what == "attn":
                    pe.wait_ge(w1_split, t + 1)
                    split_ready("w2", 0, t)
                    for i in range(TPB):
                        rows_i = slice(i * P, (i + 1) * P)
                        ins = products(m_bank[i][:, :], [((w1_hi[:, t, rows_i], w1_lo[:, t, rows_i]),
                                                          (w2t_hi[:, t, :], w2t_lo[:, t, :]))],
                                       first=t == 0, last=t == KC - 1)
                        if t == KC - 1:
                            ins.then_inc(m_done, 1)
                elif kind in ("M", "early"):
                    m = M_AT[what, b, t]
                    bank = m_free_for(m)
                    tokens = columns_of(kind, what, b)
                    tiles = tokens.stop // P
                    cols = slice(t * P, (t + 1) * P)
                    if what == "y1":
                        split_ready("x1", b, t)
                        for c in range(KC):
                            if n == 0:
                                pe.wait_ge(attn_split, c + 1)
                            ins = products(bank, [((odd_hi[:, c, cols], odd_lo[:, c, cols]),
                                                   (attn_hi[:, c, :], attn_lo[:, c, :]))],
                                           bias1 if c == KC - 1 else None, first=c == 0, last=c == KC - 1)
                    elif what in ("cl2", "cl4"):
                        if what == "cl2" and b == 0:
                            split_ready("cen", 0, 0)
                        split_ready("x" + what[-1], b, tiles - 1)
                        for c in range(KC):
                            for h, a in enumerate(clustered_in(b)):
                                ins = pe.matmul(bank[:, tokens], cen_hl[:, c, :], a[:, c, tokens],
                                                start=(c + h == 0), stop=(c == KC - 1 and h == 1))
                    elif what in ("dn2", "dn4"):
                        if what == "dn2" and n == 0:
                            split_ready("ffn", 0, KC - 1)
                        hi, lo = clustered_in(b)
                        chunks = chunks_of(kind, what, b, t)
                        ins = products(bank, [((hi[:, c, cols], lo[:, c, cols]),
                                               (ffn_hi[:, c, :], ffn_lo[:, c, :])) for c in chunks],
                                       first=0 in chunks, last=KC - 1 in chunks)
                    elif what in ("q", "k", "v"):
                        w = slice("qkv".index(what) * DH, ("qkv".index(what) + 1) * DH)
                        if kind == "early" and what == "q":
                            pe.wait_ge(late_split, 2 * KC + 2)
                        if what == "q":
                            split_ready("x3", b, tiles - 1)
                        ins = products(bank[:, tokens], [((wqkv_hi[:, c, w], wqkv_lo[:, c, w]),
                                                          (odd_hi[:, c, tokens], odd_lo[:, c, tokens]))
                                                         for c in range(KC)])
                    elif what == "sc":
                        if t == 0:
                            pe.wait_ge(*m_freed(M_AT["k", b, 0]))
                        ins = products(bank, [((q_hi[:, cols], q_lo[:, cols]), (k_hi, k_lo))])
                    elif what == "pv":
                        split_ready("v", b, 0)
                        split_ready("p", b, TPB - 1)
                        ins = products(bank, [((v_hi[:, c * P:(c + 1) * P], v_lo[:, c * P:(c + 1) * P]),
                                               (pt_hi[:, c, :], pt_lo[:, c, :])) for c in range(KC)])
                    elif what == "wo":
                        if t == 0:
                            pe.wait_ge(*m_freed(M_AT["pv", b, 0]))
                        ins = products(bank, [((o_hi[:, cols], o_lo[:, cols]), (wo_hi[:, :], wo_lo[:, :]))])
                    if kind == "M":
                        ins.then_inc(m_done, 1)
                elif kind in ("best2", "best4"):
                    j = T_AT[kind, 0, 0]
                    bank = t_free_for(j)
                    pe.wait_ge(best_done, 1 + (kind == "best4"))
                    pe.transpose(bank[0:NC, 0:P], best1[:, :], ident[:, :]).then_inc(t_done, 1)
                elif kind in ("mask2", "mask4"):
                    m = M_AT[kind, 0, 0]
                    bank = m_free_for(m)
                    pe.wait_ge(csel_done, 1 + (kind == "mask4"))
                    pe.wait_ge(onehot_done, 1)
                    pe.matmul(bank[:, :], csel[:, :], onehot[:, :], start=True, stop=True).then_inc(m_done, 1)


_INS = ["L0_attn_a_x", "L0_attn_a_w1", "L0_attn_a_w2", "L0_attn_a_b2", "L0_attn_a_sparse_mask", "L0_attn_b_Wqkv",
        "L0_attn_b_bqkv", "L0_attn_b_Wo", "L0_attn_b_bo", "L0_ffn_weight", "L0_ffn_bias", "L0_ffn_centroids",
        "L0_ffn_assignments"]


def kernel(**inputs):
    import numpy as np
    import concourse.bacc as bacc
    from concourse.bass_utils import run_bass_kernel_spmd

    nc = bacc.Bacc("TRN2", target_bir_lowering=False, num_devices=1)
    arrays, args = {}, []
    for name in _INS:
        a = np.ascontiguousarray(inputs[name])
        arrays[f"in_{name}"] = a
        args.append(nc.dram_tensor(f"in_{name}", a.shape, mybir.dt.from_np(a.dtype), kind="ExternalInput").ap())
    out = nc.dram_tensor("out", (NB, S, D), F32, kind="ExternalOutput").ap()
    program(nc, *args, out)
    r = run_bass_kernel_spmd(nc, [arrays], core_ids=[0])
    return r.results[0]["out"]
```
